# Optimizing a Trainium2 kernel written in Bass

```python
import numpy as np
import jax
import jax.numpy as jnp

def _softmax(x, axis=-1):
    return jax.nn.softmax(x, axis=axis)

def _gelu(x):
    return jax.nn.gelu(x, approximate=True)

def _silu(x):
    return jax.nn.silu(x)

def _sigmoid(x):
    return jax.nn.sigmoid(x)

def _layernorm(x, axis=-1, eps=1e-05):
    m = jnp.mean(x, axis=axis, keepdims=True)
    v = jnp.var(x, axis=axis, keepdims=True)
    return (x - m) / jnp.sqrt(v + eps)

def _scatter_add(tgt, idx, src, axis=0):
    return tgt.at[idx].add(src)

def _segment_sum(src, seg, n):
    return jax.ops.segment_sum(src, seg, n)
kernel_name = 'mk_dlrm_tower_d1_rec_r8_3c10ce'

def setup_inputs(seed: int=0):
    np.random.seed(seed)
    _w = jnp.asarray

    def _rec_inputs():
        import jax
        import jax.numpy as jnp
        _tk = jax.random.key(seed)
        dense_ctx = jax.random.normal(jax.random.fold_in(_tk, 190), (2048, 16), jnp.float32)
        ids = jnp.stack([jax.random.randint(jax.random.fold_in(_tk, 200 + f), (2048,), 0, v, jnp.int32) for f, v in enumerate([1000, 12500, 125000, 12500, 1000, 1250, 1250, 125000, 1250, 12500, 125000, 1000, 12500, 12500, 12500, 1000, 1250, 1000, 1000, 12500, 1000, 1000, 12500, 1000, 1000, 1250, 1000, 1250, 1000, 1250, 1000, 1000, 1000, 1000, 1250, 1000, 1000, 1000, 1000])], axis=1)
        tbl_0 = 0.05 * jax.random.normal(jax.random.fold_in(_tk, 500 + 0), (1000, 64), jnp.float32)
        tbl_1 = 0.05 * jax.random.normal(jax.random.fold_in(_tk, 500 + 1), (12500, 64), jnp.float32)
        tbl_2 = 0.05 * jax.random.normal(jax.random.fold_in(_tk, 500 + 2), (125000, 64), jnp.float32)
        tbl_3 = 0.05 * jax.random.normal(jax.random.fold_in(_tk, 500 + 3), (12500, 64), jnp.float32)
        tbl_4 = 0.05 * jax.random.normal(jax.random.fold_in(_tk, 500 + 4), (1000, 64), jnp.float32)
        tbl_5 = 0.05 * jax.random.normal(jax.random.fold_in(_tk, 500 + 5), (1250, 64), jnp.float32)
        tbl_6 = 0.05 * jax.random.normal(jax.random.fold_in(_tk, 500 + 6), (1250, 64), jnp.float32)
        tbl_7 = 0.05 * jax.random.normal(jax.random.fold_in(_tk, 500 + 7), (125000, 64), jnp.float32)
        tbl_8 = 0.05 * jax.random.normal(jax.random.fold_in(_tk, 500 + 8), (1250, 64), jnp.float32)
        tbl_9 = 0.05 * jax.random.normal(jax.random.fold_in(_tk, 500 + 9), (12500, 64), jnp.float32)
        tbl_10 = 0.05 * jax.random.normal(jax.random.fold_in(_tk, 500 + 10), (125000, 64), jnp.float32)
        tbl_11 = 0.05 * jax.random.normal(jax.random.fold_in(_tk, 500 + 11), (1000, 64), jnp.float32)
        tbl_12 = 0.05 * jax.random.normal(jax.random.fold_in(_tk, 500 + 12), (12500, 64), jnp.float32)
        tbl_13 = 0.05 * jax.random.normal(jax.random.fold_in(_tk, 500 + 13), (12500, 64), jnp.float32)
        tbl_14 = 0.05 * jax.random.normal(jax.random.fold_in(_tk, 500 + 14), (12500, 64), jnp.float32)
        tbl_15 = 0.05 * jax.random.normal(jax.random.fold_in(_tk, 500 + 15), (1000, 64), jnp.float32)
        tbl_16 = 0.05 * jax.random.normal(jax.random.fold_in(_tk, 500 + 16), (1250, 64), jnp.float32)
        tbl_17 = 0.05 * jax.random.normal(jax.random.fold_in(_tk, 500 + 17), (1000, 64), jnp.float32)
        tbl_18 = 0.05 * jax.random.normal(jax.random.fold_in(_tk, 500 + 18), (1000, 64), jnp.float32)
        tbl_19 = 0.05 * jax.random.normal(jax.random.fold_in(_tk, 500 + 19), (12500, 64), jnp.float32)
        tbl_20 = 0.05 * jax.random.normal(jax.random.fold_in(_tk, 500 + 20), (1000, 64), jnp.float32)
        tbl_21 = 0.05 * jax.random.normal(jax.random.fold_in(_tk, 500 + 21), (1000, 64), jnp.float32)
        tbl_22 = 0.05 * jax.random.normal(jax.random.fold_in(_tk, 500 + 22), (12500, 64), jnp.float32)
        tbl_23 = 0.05 * jax.random.normal(jax.random.fold_in(_tk, 500 + 23), (1000, 64), jnp.float32)
        tbl_24 = 0.05 * jax.random.normal(jax.random.fold_in(_tk, 500 + 24), (1000, 64), jnp.float32)
        tbl_25 = 0.05 * jax.random.normal(jax.random.fold_in(_tk, 500 + 25), (1250, 64), jnp.float32)
        tbl_26 = 0.05 * jax.random.normal(jax.random.fold_in(_tk, 500 + 26), (1000, 64), jnp.float32)
        tbl_27 = 0.05 * jax.random.normal(jax.random.fold_in(_tk, 500 + 27), (1250, 64), jnp.float32)
        tbl_28 = 0.05 * jax.random.normal(jax.random.fold_in(_tk, 500 + 28), (1000, 64), jnp.float32)
        tbl_29 = 0.05 * jax.random.normal(jax.random.fold_in(_tk, 500 + 29), (1250, 64), jnp.float32)
        tbl_30 = 0.05 * jax.random.normal(jax.random.fold_in(_tk, 500 + 30), (1000, 64), jnp.float32)
        tbl_31 = 0.05 * jax.random.normal(jax.random.fold_in(_tk, 500 + 31), (1000, 64), jnp.float32)
        tbl_32 = 0.05 * jax.random.normal(jax.random.fold_in(_tk, 500 + 32), (1000, 64), jnp.float32)
        tbl_33 = 0.05 * jax.random.normal(jax.random.fold_in(_tk, 500 + 33), (1000, 64), jnp.float32)
        tbl_34 = 0.05 * jax.random.normal(jax.random.fold_in(_tk, 500 + 34), (1250, 64), jnp.float32)
        tbl_35 = 0.05 * jax.random.normal(jax.random.fold_in(_tk, 500 + 35), (1000, 64), jnp.float32)
        tbl_36 = 0.05 * jax.random.normal(jax.random.fold_in(_tk, 500 + 36), (1000, 64), jnp.float32)
        tbl_37 = 0.05 * jax.random.normal(jax.random.fold_in(_tk, 500 + 37), (1000, 64), jnp.float32)
        tbl_38 = 0.05 * jax.random.normal(jax.random.fold_in(_tk, 500 + 38), (1000, 64), jnp.float32)
        _rk = jax.random.fold_in(_tk, 7)
        W_top1 = 0.0363456 * jax.random.normal(jax.random.fold_in(_tk, 801), (757, 512), jnp.float32)
        W_top2 = 0.0441942 * jax.random.normal(jax.random.fold_in(_tk, 802), (512, 256), jnp.float32)
        W_top3 = 0.0625 * jax.random.normal(jax.random.fold_in(_tk, 803), (256, 1), jnp.float32)
        b_top1 = jnp.zeros((512,), jnp.float32)
        b_top2 = jnp.zeros((256,), jnp.float32)
        return (dense_ctx, ids, tbl_0, tbl_1, tbl_2, tbl_3, tbl_4, tbl_5, tbl_6, tbl_7, tbl_8, tbl_9, tbl_10, tbl_11, tbl_12, tbl_13, tbl_14, tbl_15, tbl_16, tbl_17, tbl_18, tbl_19, tbl_20, tbl_21, tbl_22, tbl_23, tbl_24, tbl_25, tbl_26, tbl_27, tbl_28, tbl_29, tbl_30, tbl_31, tbl_32, tbl_33, tbl_34, tbl_35, tbl_36, tbl_37, tbl_38, W_top1, b_top1, W_top2, b_top2, W_top3)
    dense_ctx, ids, tbl_0, tbl_1, tbl_2, tbl_3, tbl_4, tbl_5, tbl_6, tbl_7, tbl_8, tbl_9, tbl_10, tbl_11, tbl_12, tbl_13, tbl_14, tbl_15, tbl_16, tbl_17, tbl_18, tbl_19, tbl_20, tbl_21, tbl_22, tbl_23, tbl_24, tbl_25, tbl_26, tbl_27, tbl_28, tbl_29, tbl_30, tbl_31, tbl_32, tbl_33, tbl_34, tbl_35, tbl_36, tbl_37, tbl_38, W_top1, b_top1, W_top2, b_top2, W_top3 = _rec_inputs()

    def _L0_rec_setup():
        import jax, jax.numpy as jnp
        import numpy as np
        NUM_FIELDS = 39
        _ROW, _COL = np.triu_indices(NUM_FIELDS, k=1)
        key = jax.random.key(seed)
        x = jax.random.normal(key, (2048, NUM_FIELDS, 64), dtype=jnp.float32)
        return {'x': x}
    _L0_rec_all = _L0_rec_setup()
    _L0_rec_in = {k: v for k, v in _L0_rec_all.items() if k in ()}
    del _L0_rec_all
    return {'dense_ctx': dense_ctx, 'ids': ids, 'tbl_0': tbl_0, 'tbl_1': tbl_1, 'tbl_2': tbl_2, 'tbl_3': tbl_3, 'tbl_4': tbl_4, 'tbl_5': tbl_5, 'tbl_6': tbl_6, 'tbl_7': tbl_7, 'tbl_8': tbl_8, 'tbl_9': tbl_9, 'tbl_10': tbl_10, 'tbl_11': tbl_11, 'tbl_12': tbl_12, 'tbl_13': tbl_13, 'tbl_14': tbl_14, 'tbl_15': tbl_15, 'tbl_16': tbl_16, 'tbl_17': tbl_17, 'tbl_18': tbl_18, 'tbl_19': tbl_19, 'tbl_20': tbl_20, 'tbl_21': tbl_21, 'tbl_22': tbl_22, 'tbl_23': tbl_23, 'tbl_24': tbl_24, 'tbl_25': tbl_25, 'tbl_26': tbl_26, 'tbl_27': tbl_27, 'tbl_28': tbl_28, 'tbl_29': tbl_29, 'tbl_30': tbl_30, 'tbl_31': tbl_31, 'tbl_32': tbl_32, 'tbl_33': tbl_33, 'tbl_34': tbl_34, 'tbl_35': tbl_35, 'tbl_36': tbl_36, 'tbl_37': tbl_37, 'tbl_38': tbl_38, 'W_top1': W_top1, 'b_top1': b_top1, 'W_top2': W_top2, 'b_top2': b_top2, 'W_top3': W_top3}

def reference(dense_ctx, ids, tbl_0, tbl_1, tbl_2, tbl_3, tbl_4, tbl_5, tbl_6, tbl_7, tbl_8, tbl_9, tbl_10, tbl_11, tbl_12, tbl_13, tbl_14, tbl_15, tbl_16, tbl_17, tbl_18, tbl_19, tbl_20, tbl_21, tbl_22, tbl_23, tbl_24, tbl_25, tbl_26, tbl_27, tbl_28, tbl_29, tbl_30, tbl_31, tbl_32, tbl_33, tbl_34, tbl_35, tbl_36, tbl_37, tbl_38, W_top1, b_top1, W_top2, b_top2, W_top3):
    import jax
    import jax.numpy as jnp

    def _L0_rec_ref(x):
        import jax, jax.numpy as jnp
        import numpy as np
        NUM_FIELDS = 39
        _ROW, _COL = np.triu_indices(NUM_FIELDS, k=1)
        s = jnp.sum(x, axis=-1)
        return s[:, _ROW] * s[:, _COL]
    e = jnp.stack([tbl_0[ids[:, 0]], tbl_1[ids[:, 1]], tbl_2[ids[:, 2]], tbl_3[ids[:, 3]], tbl_4[ids[:, 4]], tbl_5[ids[:, 5]], tbl_6[ids[:, 6]], tbl_7[ids[:, 7]], tbl_8[ids[:, 8]], tbl_9[ids[:, 9]], tbl_10[ids[:, 10]], tbl_11[ids[:, 11]], tbl_12[ids[:, 12]], tbl_13[ids[:, 13]], tbl_14[ids[:, 14]], tbl_15[ids[:, 15]], tbl_16[ids[:, 16]], tbl_17[ids[:, 17]], tbl_18[ids[:, 18]], tbl_19[ids[:, 19]], tbl_20[ids[:, 20]], tbl_21[ids[:, 21]], tbl_22[ids[:, 22]], tbl_23[ids[:, 23]], tbl_24[ids[:, 24]], tbl_25[ids[:, 25]], tbl_26[ids[:, 26]], tbl_27[ids[:, 27]], tbl_28[ids[:, 28]], tbl_29[ids[:, 29]], tbl_30[ids[:, 30]], tbl_31[ids[:, 31]], tbl_32[ids[:, 32]], tbl_33[ids[:, 33]], tbl_34[ids[:, 34]], tbl_35[ids[:, 35]], tbl_36[ids[:, 36]], tbl_37[ids[:, 37]], tbl_38[ids[:, 38]]], axis=1)
    z = _L0_rec_ref(e)
    z = z.reshape(z.shape[0], -1)
    h = jnp.concatenate([z, dense_ctx], axis=1)
    h = jnp.maximum(h @ W_top1 + b_top1, 0.0)
    h = jnp.maximum(h @ W_top2 + b_top2, 0.0)
    y = h @ W_top3
    return y

_drawn_inputs = setup_inputs


def setup_inputs(seed=0):
    import zlib

    import numpy as np

    out = dict(_drawn_inputs(seed))
    spreads = {'b_top1': (0.0, 0.1), 'b_top2': (0.0, 0.1)}
    factors = {}
    for name, (base, spread) in spreads.items():
        noise = np.random.default_rng([zlib.crc32(name.encode()), seed]).standard_normal(out[name].shape)
        drawn = base * np.exp(spread * noise) if base else spread * noise
        out[name] = jnp.asarray(drawn.astype(out[name].dtype))
    for name, factor in factors.items():
        out[name] = (out[name] * factor).astype(out[name].dtype)
    return out
```

```python
import concourse.bass as bass
from concourse import mybir
from contextlib import ExitStack

VOCABS = [1000, 12500, 125000, 12500, 1000, 1250, 1250, 125000, 1250, 12500, 125000, 1000, 12500,
          12500, 12500, 1000, 1250, 1000, 1000, 12500, 1000, 1000, 12500, 1000, 1000, 1250, 1000,
          1250, 1000, 1250, 1000, 1000, 1000, 1000, 1250, 1000, 1000, 1000, 1000]
BATCH = 2048
DIM = 64
P = 128
NF = len(VOCABS)
NPAIR = NF * (NF - 1) // 2
NDENSE = 16
H1, H2 = 512, 256

R = 32
KINDS = [dict(vocab=1000, q=32, fpg=4), dict(vocab=1250, q=40, fpg=3)]
A_FIELDS = [f for f, v in enumerate(VOCABS) if v == 1000]
B_FIELDS = [f for f, v in enumerate(VOCABS) if v == 1250]
SMALL = A_FIELDS + B_FIELDS
NS = len(SMALL)
GROUPS = []
for fields, kind in ((A_FIELDS, KINDS[0]), (B_FIELDS, KINDS[1])):
    for first in range(0, len(fields), kind["fpg"]):
        n = min(kind["fpg"], len(fields) - first)
        GROUPS.append((kind["q"], n, len(fields) * 0 + first + (0 if kind is KINDS[0] else len(A_FIELDS)),
                       n * kind["q"]))
NG = len(GROUPS)
NGA = sum(g[0] == 32 for g in GROUPS)
MEDIUM = [f for f, v in enumerate(VOCABS) if v == 12500]
MR, MQ = 100, 125
DENSE_MEDIUM = MEDIUM[:1]
GATHERED = MEDIUM[1:] + [f for f, v in enumerate(VOCABS) if v == 125000]
NGAT = len(GATHERED)
ORDER = SMALL + DENSE_MEDIUM + GATHERED
NL = NS + 1
POS = {f: i for i, f in enumerate(ORDER)}

TILES = BATCH // P
CHUNK = 256
TPC = CHUNK // P
CHUNKS = BATCH // CHUNK
SLOTS = 4
RING = 4
KC = (NPAIR + NDENSE + P - 1) // P
LAST_PAIRS = NPAIR - (KC - 1) * P
LAST_K = LAST_PAIRS + NDENSE
PARTS = 3
SK = PARTS * NF
ROUND = 12582912.0


def tower(nc, ids_sample, ids_field, rows_a, rows_b, medium, gathered, dense_t, w1, b1, w2, b2, w3,
          c_field, c_part, c_pow2, c_onehot, c_select, c_ident, y_out):
    fp32, bf16, fp16, i32 = mybir.dt.float32, mybir.dt.bfloat16, mybir.dt.float16, mybir.dt.int32
    u32 = mybir.dt.uint32
    ALU = mybir.AluOpType
    ACT = mybir.ActivationFunctionType
    AX = mybir.AxisListType

    ctx = ExitStack()
    with ctx:
        def sb(name, shape, dt):
            return ctx.enter_context(nc.sbuf_tensor(name, shape, dt))

        def sem(name):
            return ctx.enter_context(nc.semaphore(name))

        ids_s = sb("ids_s", [P, TILES, NF], i32)
        ids_f = sb("ids_f", [NL, BATCH], i32)
        field_c = sb("field_c", [NL, 2], fp32)
        part_c = sb("part_c", [P, 12], fp32)
        pow2 = sb("pow2", [P, 7], i32)
        onehot_w = sb("onehot_w", [65, NG + 1, P], fp16)
        select_w = sb("select_w", [SK, 2, KC * P], bf16)
        ident = sb("ident", [P, P], fp32)
        rows = sb("rows", [P, RING, R * DIM], fp32)
        mrows = sb("mrows", [MQ, MR * DIM], fp32)
        sums = sb("sums", [P, NG * R + MR], fp32)
        rest = sb("rest", [P, NG * R + MR], fp32)
        sum_parts = sb("sum_parts", [P, PARTS, NG * R + MR], bf16)
        blocks = sb("blocks", [P, PARTS, NG, P], bf16)
        quot = sb("quot", [65, BATCH], fp16)
        hot = sb("hot", [P, NG + 1, BATCH], bf16)
        mquot = sb("mquot", [P, 2, TILES], fp32)
        mlow = sb("mlow", [P, TILES], i32)
        bits = sb("bits", [P, 2, 2, NS, 5], i32)
        mbits = sb("mbits", [P, 2, 2, 7], i32)
        looked = sb("looked", [P, TILES, NL], fp32)
        index = sb("index", [P, SLOTS, TPC, NGAT], i32)
        grows = sb("grows", [P, SLOTS, TPC, NGAT, DIM], fp32)
        s_all = sb("s_all", [P, TPC, PARTS, NF], fp32)
        cut_a = sb("cut_a", [SK, CHUNK], bf16)
        rest_a = sb("rest_a", [SK, CHUNK], fp32)
        cut_b = sb("cut_b", [SK, CHUNK], bf16)
        s_parts = sb("s_parts", [SK, CHUNK], bf16)
        rowv = sb("rowv", [P, 2, CHUNK], fp32)
        z = sb("z", [P, KC - 1, CHUNK], fp32)
        zlast = sb("zlast", [LAST_K, BATCH], fp32)
        w1_s = sb("w1_s", [P, KC, H1], fp32)
        w2_s = sb("w2_s", [P, H1 // P, H2], fp32)
        w3_s = sb("w3_s", [P, H2 // P], fp32)
        b1_s = sb("b1_s", [P, H1 // P], fp32)
        b2_s = sb("b2_s", [P, H2 // P], fp32)
        h1_s = sb("h1_s", [P, H1 // P, CHUNK], fp32)
        h2_s = sb("h2_s", [P, H2 // P, CHUNK], fp32)
        y_s = sb("y_s", [1, CHUNK], fp32)

        ps = ctx.enter_context(nc.psum_tensor("ps", [P, 8, 512], fp32))
        X = [ps[:, 4 * s:4 * s + 4, :].rearrange("p (t b) n -> p t (b n)", t=2) for s in range(2)]
        B_ROW, B_COL, B_SUM, B_H2 = 4, 5, 6, 7

        ld_ids = sem("ld_ids")
        ld_ids_s = sem("ld_ids_s")
        ld_field = sem("ld_field")
        ld_part = sem("ld_part")
        ld_pow2 = sem("ld_pow2")
        ld_onehot = sem("ld_onehot")
        ld_select = sem("ld_select")
        ld_ident = sem("ld_ident")
        ld_rows = [sem(f"ld_rows{g}") for g in range(NG)]
        ld_mrows = [sem(f"ld_mrows{i}") for i in range(2)]
        ld_w = sem("ld_w")
        ld_dense = sem("ld_dense")
        quot_clear = sem("quot_clear")
        sums_clear = sem("sums_clear")
        prep = sem("prep")
        quot_ready = sem("quot_ready")
        bcast_ready = sem("bcast_ready")
        hot_ready = sem("hot_ready")
        mhot_ready = sem("mhot_ready")
        blocks_ready = sem("blocks_ready")
        looked_mm = sem("looked_mm")
        bits_ready = sem("bits_ready")
        small_step = sem("small_step")
        medium_step = sem("medium_step")
        looked_ready = [sem(f"looked_ready{u}") for u in range(2)]
        index_ready = sem("index_ready")
        gathered_in = [sem(f"gathered_in{s}") for s in range(SLOTS)]
        grows_used = [sem(f"grows_used{s}") for s in range(SLOTS)]
        rows_used = sem("rows_used")
        s_ready = sem("s_ready")
        st_ready = sem("st_ready")
        cut_a_ready = sem("cut_a_ready")
        rest_a_ready = sem("rest_a_ready")
        cut_b_ready = sem("cut_b_ready")
        parts_ready = sem("parts_ready")
        select_ready = sem("select_ready")
        rowv_ready = sem("rowv_ready")
        z_ready = sem("z_ready")
        h1_ready = sem("h1_ready")
        h1_relu = sem("h1_relu")
        h2_ready = sem("h2_ready")
        h2_relu = sem("h2_relu")
        y_ready = sem("y_ready")
        y_copied = sem("y_copied")
        y_stored = sem("y_stored")

        NW = 7
        QB = BATCH // 512
        PAIRS = TILES // 2
        NZ = (KC + 1) // 2

        block = ctx.enter_context(nc.Block())


        @block.sync
        def _(sp):
            nc.sync.sem_inc(y_stored, 16)
            sp.dma_start(ids_f[:, :], ids_field).then_inc(ld_ids, 16)
            sp.dma_start(field_c[:, :], c_field).then_inc(ld_field, 16)
            sp.dma_start(onehot_w[:, :, :], c_onehot).then_inc(ld_onehot, 16)
            sp.dma_start(part_c[:, :], c_part).then_inc(ld_part, 16)
            for g, (q, n, first, used) in enumerate(GROUPS):
                src = rows_a[g, :, :] if q == 32 else rows_b[(first - len(A_FIELDS)) * q:(first - len(A_FIELDS) + n) * q, :]
                if g >= RING:
                    sp.wait_ge(rows_used, g - RING + 1)
                sp.dma_start(rows[0:used, g % RING, :], src).then_inc(ld_rows[g], 16)
            half = MR // 2 * DIM
            for i in range(2):
                sp.dma_start(mrows[:, i * half:(i + 1) * half], medium[:, i * half:(i + 1) * half]).then_inc(ld_mrows[i], 16)
            with nc.sync.Fori(0, CHUNKS) as c:
                sp.wait_ge(y_copied, c + 2)
                sp.dma_start(y_out[:, bass.ds(c * CHUNK, CHUNK)], y_s[:, :]).then_inc(y_stored, 16)
            sp.wait_ge(y_stored, 16 * CHUNKS + 16)

        @block.gpsimd
        def _(pool):
            pool.wait_ge(ld_ids_s, 16)
            with nc.gpsimd.Fori(0, CHUNKS // SLOTS) as it:
                for s in range(SLOTS):
                    pool.wait_ge(grows_used[s], it + 1)
                    nc.gpsimd.tensor_copy(
                        index[:, s, :, :], ids_s[:, bass.ds(it * (SLOTS * TPC) + s * TPC, TPC), NL:NF]
                    ).then_inc(index_ready, 1)
                    pool.wait_ge(index_ready, s + 1)
                    for t in range(TPC):
                        for j in range(NGAT):
                            nc.gpsimd.indirect_dma_start(
                                out=grows[:, s, t, j, :], out_offset=None, in_=gathered[j],
                                in_offset=bass.IndirectOffsetOnAxis(ap=index[:, s, t, j:j + 1].bitcast(u32), axis=0),
                            ).then_inc(gathered_in[s], 16)
                nc.gpsimd.sem_clear(index_ready)

        @block.scalar
        def _(act):
            nc.scalar.sem_inc(hot_ready, 1)
            nc.scalar.sem_inc(y_copied, 1)
            act.dma_start(ids_s[:, :, :], ids_sample).then_inc(ld_ids_s, 16)
            act.dma_start(pow2[:, :], c_pow2).then_inc(ld_pow2, 16)
            act.dma_start(ident[:, :], c_ident).then_inc(ld_ident, 16)
            act.dma_start(select_w[:, :, :], c_select).then_inc(ld_select, 16)
            act.dma_start(w1_s[:, 0:KC - 1, :], w1[0:(KC - 1) * P, :].rearrange("(c p) n -> p c n", p=P)).then_inc(ld_w, 16)
            act.dma_start(w1_s[0:LAST_K, KC - 1, :], w1[(KC - 1) * P:NPAIR + NDENSE, :]).then_inc(ld_w, 16)
            act.dma_start(w2_s[:, :, :], w2.rearrange("(c p) n -> p c n", p=P)).then_inc(ld_w, 16)
            act.dma_start(w3_s[:, :], w3).then_inc(ld_w, 16)
            act.dma_start(b1_s[:, :], b1).then_inc(ld_w, 16)
            act.dma_start(b2_s[:, :], b2).then_inc(ld_w, 16)
            act.dma_start(zlast[LAST_PAIRS:LAST_K, :], dense_t).then_inc(ld_w, 16)
            with nc.scalar.Fori(0, QB) as b:
                for g, (q, n, first, used) in enumerate(GROUPS):
                    act.wait_ge(bcast_ready, b * (NG + 1) + g + 1)
                    nc.scalar.activation(hot[0:used, g, bass.ds(b * 512, 512)], ps[0:used, g % 7, :],
                                         ACT.Relu).then_inc(hot_ready, 1)
            act.wait_ge(ld_w, 16 * NW)
            with nc.scalar.Fori(0, CHUNKS) as c:
                act.wait_ge(st_ready, c + 2)
                nc.scalar.activation(cut_a[:, :], ps[0:SK, B_SUM, 0:CHUNK], ACT.Copy).then_inc(cut_a_ready, 1)
                act.wait_ge(rest_a_ready, c + 1)
                nc.scalar.activation(cut_b[:, :], rest_a[:, :], ACT.Copy).then_inc(cut_b_ready, 1)
                for k in range(NZ):
                    act.wait_ge(select_ready, c * NZ + k + 1)
                    if k > 0:
                        act.wait_ge(z_ready, c * NZ + k)
                    if k < NZ - 1:
                        nc.scalar.activation(rowv[:, :, :], ps[:, B_ROW, :].rearrange("p (a n) -> p a n", a=2),
                                             ACT.Copy).then_inc(rowv_ready, 2)
                    else:
                        nc.scalar.activation(rowv[:, 0, :], ps[:, B_ROW, 0:CHUNK], ACT.Copy).then_inc(rowv_ready, 1)
                        nc.scalar.activation(rowv[0:LAST_PAIRS, 1, :], ps[0:LAST_PAIRS, B_ROW, CHUNK:],
                                             ACT.Copy).then_inc(rowv_ready, 1)
                for m in range(H1 // P):
                    act.wait_ge(h1_ready, c * (H1 // P) + m + 1)
                    nc.scalar.activation(h1_s[:, m, :], ps[:, m, 0:CHUNK], ACT.Relu,
                                         bias=b1_s[:, m:m + 1]).then_inc(h1_relu, 1)
                for m in range(H2 // P):
                    act.wait_ge(h2_ready, c * (H2 // P) + m + 1)
                    nc.scalar.activation(h2_s[:, m, :], ps[:, B_H2 if m == 0 else B_COL, 0:CHUNK], ACT.Relu,
                                         bias=b2_s[:, m:m + 1]).then_inc(h2_relu, 1)
                act.wait_ge(y_ready, c + 1)
                act.wait_ge(y_stored, (c + 1) * 16)
                nc.scalar.activation(y_s[:, :], ps[0:1, B_ROW, 0:CHUNK],
                                     ACT.Copy).then_inc(y_copied, 1)

        @block.vector
        def _(dve):
            chain = [0]

            def link(ins):
                chain[0] += 1
                ins.then_inc(prep, 1)
                dve.wait_ge(prep, chain[0])

            nc.vector.sem_inc(mhot_ready, 1)
            for s in range(SLOTS):
                nc.vector.sem_inc(grows_used[s], 1)
            for u in range(2):
                nc.vector.sem_inc(looked_ready[u], 1)
            nc.vector.memset(quot[:, :].bitcast(fp32), 0.0).then_inc(quot_clear, 1)
            nc.vector.memset(sums[:, :], 0.0).then_inc(sums_clear, 1)
            dve.wait_ge(quot_clear, 1)
            nc.vector.memset(quot[64:65, :], 1.0).then_inc(quot_ready, 1)
            dve.wait_ge(ld_ids, 16)
            dve.wait_ge(ld_field, 16)
            link(nc.vector.tensor_scalar(ids_f[:, :].bitcast(fp32), ids_f[:, :], field_c[:, 0:1], field_c[:, 1:2],
                                         ALU.subtract, ALU.mult))
            link(nc.vector.tensor_scalar(quot[0:NL, :], ids_f[:, :].bitcast(fp32), ROUND, ROUND, ALU.add, ALU.subtract))
            nc.vector.tensor_tensor(quot[32:32 + NS, :], quot[0:NS, :], quot[0:NS, :], ALU.mult).then_inc(quot_ready, 1)
            dve.wait_ge(ld_ids_s, 16)
            mid = ids_s[:, :, NS]
            link(nc.vector.tensor_scalar(mquot[:, 0, :], mid, (MR - 1) / 2, 1.0 / MR, ALU.subtract, ALU.mult))
            link(nc.vector.tensor_scalar(mquot[:, 1, :], mquot[:, 0, :], ROUND, ROUND, ALU.add, ALU.subtract))
            link(nc.vector.scalar_tensor_tensor(out=mlow[:, :], in0=mquot[:, 1, :], scalar=-float(MR), in1=mid,
                                                op0=ALU.mult, op1=ALU.add))
            dve.wait_ge(ld_part, 16)

            def one_hot_medium(b):
                dve.wait_ge(bcast_ready, (b + 1) * (NG + 1))
                nc.vector.tensor_scalar(hot[0:MQ, NG, b * 512:(b + 1) * 512], ps[0:MQ, 7, :], part_c[0:MQ, 0:1],
                                        None, ALU.is_equal).then_inc(mhot_ready, 1)

            dve.wait_ge(sums_clear, 1)
            for g, (q, n, first, used) in enumerate(GROUPS):
                dve.wait_ge(ld_rows[g], 16)
                ins = nc.vector.tensor_reduce(sums[0:used, g * R:(g + 1) * R],
                                              rows[0:used, g % RING, :].rearrange("p (r d) -> p r d", d=DIM), AX.X, ALU.add).then_inc(rows_used, 1)
                if g % 2:
                    one_hot_medium(g // 2)
            for i in range(2):
                dve.wait_ge(ld_mrows[i], 16)
                h = MR // 2
                ins = nc.vector.tensor_reduce(
                    sums[0:MQ, NG * R + i * h:NG * R + (i + 1) * h],
                    mrows[:, i * h * DIM:(i + 1) * h * DIM].rearrange("p (r d) -> p r d", d=DIM), AX.X, ALU.add)
            link(ins)
            link(nc.vector.tensor_copy(sum_parts[:, 0, :], sums[:, :]))
            link(nc.vector.tensor_tensor(rest[:, :], sums[:, :], sum_parts[:, 0, :], ALU.subtract))
            link(nc.vector.tensor_copy(sum_parts[:, 1, :], rest[:, :]))
            link(nc.vector.tensor_tensor(sum_parts[:, 2, :], rest[:, :], sum_parts[:, 1, :], ALU.subtract))
            small = sum_parts[:, :, 0:NG * R].rearrange("p a (g r) -> p a g r", r=R)
            for f in range(4):
                ins = nc.vector.tensor_scalar(blocks[:, :, 0:NGA, f * R:(f + 1) * R], small[:, :, 0:NGA, :],
                                              part_c[:, 1 + f:2 + f], None, ALU.mult)
            for f in range(3):
                ins = nc.vector.tensor_scalar(blocks[:, :, NGA:NG, f * R:(f + 1) * R], small[:, :, NGA:NG, :],
                                              part_c[:, 5 + f:6 + f], None, ALU.mult)
            ins.then_inc(blocks_ready, 1)
            dve.wait_ge(ld_pow2, 16)

            with nc.vector.Fori(0, PAIRS // 2) as i:
                for u in range(2):
                    nc.vector.tensor_tensor(
                        bits[:, u, :, :, :],
                        ids_s[:, bass.ds(i * 4 + 2 * u, 2), 0:NS].unsqueeze(3).broadcast_to([P, 2, NS, 5]),
                        pow2[:, 0:5].unsqueeze(1).unsqueeze(1).broadcast_to([P, 2, NS, 5]),
                        ALU.bitwise_and).then_inc(bits_ready, 1)
                    dve.wait_ge(looked_mm, i * 2 + u + 1)
                    nc.vector.tensor_tensor(
                        mbits[:, u, :, :],
                        mlow[:, bass.ds(i * 4 + 2 * u, 2)].unsqueeze(2).broadcast_to([P, 2, 7]),
                        pow2[:, :].unsqueeze(1).broadcast_to([P, 2, 7]),
                        ALU.bitwise_and).then_inc(bits_ready, 1)
                    dve.wait_ge(bits_ready, 2 * u + 2)
                    x = X[u][:, :, 0:NS * R].rearrange("p t (f r) -> p t f r", r=R)
                    xm = X[u][:, :, NS * R:NS * R + MR]
                    for step in range(7):
                        k = 64 >> step
                        n = min(k, MR - k)
                        if step > 0:
                            dve.wait_ge(medium_step, u * 7 + step)
                        nc.vector.copy_predicated(
                            xm[:, :, 0:n], mbits[:, u, :, 6 - step:7 - step].broadcast_to([P, 2, n]),
                            xm[:, :, k:k + n]).then_inc(medium_step, 1)
                        if step < 5:
                            k = 16 >> step
                            if step > 0:
                                dve.wait_ge(small_step, u * 5 + step)
                            nc.vector.copy_predicated(
                                x[:, :, :, 0:k], bits[:, u, :, :, 4 - step:5 - step].broadcast_to([P, 2, NS, k]),
                                x[:, :, :, k:2 * k]).then_inc(small_step, 1)
                    dve.wait_ge(small_step, u * 5 + 5)
                    nc.vector.tensor_copy(looked[:, bass.ds(i * 4 + 2 * u, 2), 0:NS],
                                          x[:, :, :, 0]).then_inc(looked_ready[u], 1)
                    dve.wait_ge(medium_step, u * 7 + 7)
                    nc.vector.tensor_copy(looked[:, bass.ds(i * 4 + 2 * u, 2), NS:NL],
                                          xm[:, :, 0:1]).then_inc(looked_ready[u], 1)
                for step_sem in (bits_ready, small_step, medium_step):
                    nc.vector.sem_clear(step_sem)

            for u in range(2):
                dve.wait_ge(looked_ready[u], PAIRS + 1)
            with nc.vector.Fori(0, CHUNKS // SLOTS) as it:
                for s in range(SLOTS):
                    c = it * SLOTS + s
                    dve.wait_ge(gathered_in[s], (it + 1) * (16 * TPC * NGAT))
                    dve.wait_ge(st_ready, c + 1)
                    nc.vector.tensor_reduce(s_all[:, :, 0, NL:NF], grows[:, s, :, :, :], AX.X, ALU.add).then_inc(grows_used[s], 1)
                    ins = nc.vector.tensor_copy(s_all[:, :, 0, 0:NL], looked[:, bass.ds(it * (SLOTS * TPC) + s * TPC, TPC), :])
                    ins.then_inc(s_ready, 1)
                    dve.wait_ge(s_ready, c * 3 + 1)
                    dve.wait_ge(grows_used[s], it + 2)
                    for a in (1, 2):
                        nc.vector.tensor_copy(s_all[:, :, a, :], s_all[:, :, 0, :]).then_inc(s_ready, 1)
                    dve.wait_ge(cut_a_ready, c + 1)
                    nc.vector.scalar_tensor_tensor(out=rest_a[:, :], in0=cut_a[:, :], scalar=part_c[0:SK, 8:9],
                                                   in1=ps[0:SK, B_SUM, 0:CHUNK], op0=ALU.mult,
                                                   op1=ALU.add).then_inc(rest_a_ready, 1)
                    dve.wait_ge(cut_b_ready, c + 1)
                    nc.vector.scalar_tensor_tensor(out=s_parts[:, :], in0=cut_b[:, :], scalar=part_c[0:SK, 9:10],
                                                   in1=rest_a[:, :], op0=ALU.mult, op1=ALU.add).then_inc(parts_ready, 1)
                    for k in range(NZ):
                        dve.wait_ge(rowv_ready, (c * NZ + k + 1) * 2)
                        if k < NZ - 1:
                            nc.vector.tensor_tensor(z[:, 2 * k:2 * k + 2, :], rowv[:, :, :],
                                                    ps[:, B_COL, :].rearrange("p (a n) -> p a n", a=2),
                                                    ALU.mult).then_inc(z_ready, 1)
                        else:
                            nc.vector.tensor_tensor(z[:, 2 * k, :], rowv[:, 0, :], ps[:, B_COL, 0:CHUNK], ALU.mult)
                            nc.vector.tensor_tensor(zlast[0:LAST_PAIRS, bass.ds(c * CHUNK, CHUNK)],
                                                    rowv[0:LAST_PAIRS, 1, :], ps[0:LAST_PAIRS, B_COL, CHUNK:],
                                                    ALU.mult).then_inc(z_ready, 1)

        @block.tensor
        def _(pe):
            nc.tensor.sem_inc(st_ready, 1)
            pe.wait_ge(ld_onehot, 16)
            pe.wait_ge(quot_ready, 2)
            with nc.tensor.Fori(0, QB) as b:
                for g, (q, n, first, used) in enumerate(GROUPS):
                    if g == 0:
                        pe.wait_ge(hot_ready, b * NG + 1)
                    elif g >= 7:
                        pe.wait_ge(hot_ready, b * NG + g - 5)
                    nc.tensor.matmul(ps[0:used, g % 7, :], onehot_w[:, g, 0:used], quot[:, bass.ds(b * 512, 512)],
                                     start=True, stop=True).then_inc(bcast_ready, 1)
                pe.wait_ge(mhot_ready, b + 1)
                nc.tensor.matmul(ps[0:MQ, 7, :], onehot_w[:, NG, 0:MQ], quot[:, bass.ds(b * 512, 512)],
                                 start=True, stop=True).then_inc(bcast_ready, 1)
            pe.wait_ge(blocks_ready, 1)
            pe.wait_ge(hot_ready, QB * NG + 1)
            pe.wait_ge(mhot_ready, QB + 1)
            with nc.tensor.Fori(0, PAIRS // 2) as i:
                for u in range(2):
                    pe.wait_ge(looked_ready[u], i * 2 + 1)
                    for t in range(2):
                        at = i * (4 * P) + (2 * u + t) * P
                        for g, (q, n, first, used) in enumerate(GROUPS):
                            for a in range(PARTS):
                                nc.tensor.matmul(X[u][:, t, first * R:(first + n) * R],
                                                 hot[0:used, g, bass.ds(at, P)], blocks[0:used, a, g, 0:n * R],
                                                 start=a == 0, stop=a == PARTS - 1)
                        for a in range(PARTS):
                            ins = nc.tensor.matmul(X[u][:, t, NS * R:NS * R + MR], hot[0:MQ, NG, bass.ds(at, P)],
                                                   sum_parts[0:MQ, a, NG * R:], start=a == 0, stop=a == PARTS - 1)
                    ins.then_inc(looked_mm, 1)
            for u in range(2):
                pe.wait_ge(looked_ready[u], PAIRS + 1)
            pe.wait_ge(ld_ident, 16)
            pe.wait_ge(ld_select, 16)
            pe.wait_ge(ld_w, 16 * NW)
            with nc.tensor.Fori(0, CHUNKS) as c:
                pe.wait_ge(s_ready, (c + 1) * 3)
                for t in range(TPC):
                    ins = nc.tensor.matmul(ps[0:SK, B_SUM, t * P:(t + 1) * P],
                                           s_all[:, t, :, :].rearrange("p a f -> p (a f)"), ident[:, :],
                                           start=True, stop=True)
                ins.then_inc(st_ready, 1)
                pe.wait_ge(parts_ready, c + 1)

                def select(k):
                    if k == 0:
                        pe.wait_ge(y_copied, c + 1)
                    else:
                        pe.wait_ge(z_ready, c * NZ + k)
                    for side, bank in ((0, B_ROW), (1, B_COL)):
                        for a in range(2):
                            kc = 2 * k + a
                            m = P if kc < KC - 1 else LAST_PAIRS
                            ins = nc.tensor.matmul(ps[0:m, bank, a * CHUNK:(a + 1) * CHUNK],
                                                   select_w[:, side, kc * P:kc * P + m], s_parts[:, :],
                                                   start=True, stop=True)
                    ins.then_inc(select_ready, 1)

                select(0)
                for k in range(NZ):
                    if k + 1 < NZ:
                        select(k + 1)
                    pe.wait_ge(z_ready, c * NZ + k + 1)
                    for a in range(2):
                        kc = 2 * k + a
                        for m in range(H1 // P):
                            if kc < KC - 1:
                                ins = nc.tensor.matmul(ps[:, m, 0:CHUNK], w1_s[:, kc, m * P:(m + 1) * P], z[:, kc, :],
                                                       start=kc == 0, stop=False)
                            else:
                                nc.tensor.matmul(ps[:, m, 0:CHUNK], w1_s[0:LAST_K, kc, m * P:(m + 1) * P],
                                                 zlast[:, bass.ds(c * CHUNK, CHUNK)],
                                                 start=False, stop=True).then_inc(h1_ready, 1)
                for m in range(H2 // P):
                    for k in range(H1 // P):
                        if m == 0:
                            pe.wait_ge(h1_relu, c * (H1 // P) + k + 1)
                        ins = nc.tensor.matmul(ps[:, B_H2 if m == 0 else B_COL, 0:CHUNK], w2_s[:, k, m * P:(m + 1) * P],
                                               h1_s[:, k, :], start=k == 0, stop=k == H1 // P - 1)
                    ins.then_inc(h2_ready, 1)
                for k in range(H2 // P):
                    pe.wait_ge(h2_relu, c * (H2 // P) + k + 1)
                    ins = nc.tensor.matmul(ps[0:1, B_ROW, 0:CHUNK], w3_s[:, k:k + 1], h2_s[:, k, :],
                                           start=k == 0, stop=k == H2 // P - 1)
                ins.then_inc(y_ready, 1)


def kernel(**inputs):
    import numpy as np
    import ml_dtypes
    import concourse.bacc as bacc
    from concourse.bass_utils import run_bass_kernel_spmd

    f32 = np.float32
    arrays = {}
    ids = np.ascontiguousarray(inputs["ids"])[:, ORDER]
    arrays["ids_sample"] = np.ascontiguousarray(ids.reshape(TILES, P, NF).transpose(1, 0, 2))
    arrays["ids_field"] = np.ascontiguousarray(ids[:, :NL].T)

    def filled(f, rows):
        table = np.asarray(inputs[f"tbl_{f}"])
        return np.concatenate([table, table[:rows - table.shape[0]]]).reshape(-1, R * DIM)

    arrays["rows_a"] = np.concatenate([filled(f, 32 * R) for f in A_FIELDS]).reshape(NGA, P, R * DIM)
    arrays["rows_b"] = np.concatenate([filled(f, 40 * R) for f in B_FIELDS])
    arrays["medium"] = np.asarray(inputs[f"tbl_{DENSE_MEDIUM[0]}"]).reshape(MQ, MR * DIM)
    for j, f in enumerate(GATHERED):
        arrays[f"gathered_{j}"] = np.asarray(inputs[f"tbl_{f}"])
    arrays["dense_t"] = np.ascontiguousarray(np.asarray(inputs["dense_ctx"]).T)
    arrays["w1"] = np.asarray(inputs["W_top1"])
    arrays["b1"] = np.ascontiguousarray(np.asarray(inputs["b_top1"]).reshape(H1 // P, P).T)
    arrays["w2"] = np.asarray(inputs["W_top2"])
    arrays["b2"] = np.ascontiguousarray(np.asarray(inputs["b_top2"]).reshape(H2 // P, P).T)
    arrays["w3"] = np.ascontiguousarray(np.asarray(inputs["W_top3"]).reshape(H2 // P, P).T)

    c_field = np.zeros((NL, 2), f32)
    c_field[:, 0], c_field[:, 1] = (R - 1) / 2, 1 / R
    c_field[NS:, 0], c_field[NS:, 1] = (MR - 1) / 2, 1 / MR
    part = np.arange(P)
    c_part = np.zeros((P, 12), f32)
    c_part[:, 0] = part
    for k in range(4):
        c_part[:, 1 + k] = part // 32 == k
    for k in range(3):
        c_part[:, 5 + k] = part // 40 == k
    c_part[:, 8] = -1.0 * (part >= NF)
    c_part[:, 9] = -1.0 * (part >= 2 * NF)
    c_pow2 = np.tile(2 ** np.arange(7, dtype=np.int32), (P, 1)).astype(np.int32)
    c_onehot = np.zeros((65, NG + 1, P), np.float16)
    for g, (q, n, first, used) in enumerate(GROUPS):
        for p in range(used):
            h = p % q
            c_onehot[first + p // q, g, p] = 2 * h
            c_onehot[32 + first + p // q, g, p] = -1
            c_onehot[64, g, p] = 1 - h * h
    c_onehot[NS, NG, :] = 1
    c_select = np.zeros((PARTS, NF, 2, KC * P), f32)
    rows, cols = np.triu_indices(NF, k=1)
    for n, (i, j) in enumerate(zip(rows, cols)):
        c_select[:, POS[i], 0, n] = 1
        c_select[:, POS[j], 1, n] = 1
    arrays["c_field"], arrays["c_part"], arrays["c_pow2"], arrays["c_onehot"] = c_field, c_part, c_pow2, c_onehot
    arrays["c_select"] = c_select.reshape(SK, 2, KC * P).astype(ml_dtypes.bfloat16)
    arrays["c_ident"] = np.eye(P, dtype=f32)

    nc = bacc.Bacc("TRN2", target_bir_lowering=False, num_devices=1)
    ap = {n: nc.dram_tensor(n, a.shape, mybir.dt.from_np(a.dtype), kind="ExternalInput").ap() for n, a in arrays.items()}
    y = nc.dram_tensor("y_out", (1, BATCH), mybir.dt.float32, kind="ExternalOutput").ap()
    tower(nc, ap["ids_sample"], ap["ids_field"], ap["rows_a"], ap["rows_b"], ap["medium"],
          [ap[f"gathered_{j}"] for j in range(NGAT)], ap["dense_t"], ap["w1"], ap["b1"], ap["w2"], ap["b2"],
          ap["w3"], ap["c_field"], ap["c_part"], ap["c_pow2"], ap["c_onehot"], ap["c_select"], ap["c_ident"], y)
    r = run_bass_kernel_spmd(nc, [arrays], core_ids=[0])
    return r.results[0]["y_out"].reshape(BATCH, 1)
```

```python
import concourse.bass as bass
from concourse import mybir
from contextlib import ExitStack

VOCABS = [1000, 12500, 125000, 12500, 1000, 1250, 1250, 125000, 1250, 12500, 125000, 1000, 12500,
          12500, 12500, 1000, 1250, 1000, 1000, 12500, 1000, 1000, 12500, 1000, 1000, 1250, 1000,
          1250, 1000, 1250, 1000, 1000, 1000, 1000, 1250, 1000, 1000, 1000, 1000]
BATCH = 2048
DIM = 64
P = 128
NF = len(VOCABS)
NPAIR = NF * (NF - 1) // 2
NDENSE = 16
H1, H2 = 512, 256

R = 32
KINDS = [dict(vocab=1000, q=32, fpg=4), dict(vocab=1250, q=40, fpg=3)]
A_FIELDS = [f for f, v in enumerate(VOCABS) if v == 1000]
B_FIELDS = [f for f, v in enumerate(VOCABS) if v == 1250]
SMALL = A_FIELDS + B_FIELDS
NS = len(SMALL)
GROUPS = []
for fields, kind in ((A_FIELDS, KINDS[0]), (B_FIELDS, KINDS[1])):
    for first in range(0, len(fields), kind["fpg"]):
        n = min(kind["fpg"], len(fields) - first)
        GROUPS.append((kind["q"], n, len(fields) * 0 + first + (0 if kind is KINDS[0] else len(A_FIELDS)),
                       n * kind["q"]))
NG = len(GROUPS)
NGA = sum(g[0] == 32 for g in GROUPS)
MEDIUM = [f for f, v in enumerate(VOCABS) if v == 12500]
MR, MQ = 100, 125
DENSE_MEDIUM = MEDIUM[:1]
GATHERED = MEDIUM[1:] + [f for f, v in enumerate(VOCABS) if v == 125000]
NGAT = len(GATHERED)
ORDER = SMALL + DENSE_MEDIUM + GATHERED
NL = NS + 1
POS = {f: i for i, f in enumerate(ORDER)}

TILES = BATCH // P
CHUNK = 256
TPC = CHUNK // P
CHUNKS = BATCH // CHUNK
SLOTS = 2
RING = 4
KC = (NPAIR + NDENSE + P - 1) // P
LAST_PAIRS = NPAIR - (KC - 1) * P
LAST_K = LAST_PAIRS + NDENSE
PARTS = 3
QK = 64 + NS
SK = PARTS * NF
ROUND = 12582912.0


def tower(nc, ids_sample, ids_field, rows_a, rows_b, medium, gathered, dense_t, w1, b1, w2, b2, w3,
          c_field, c_part, c_pow2, c_onehot, c_select, c_ident, y_out):
    fp32, bf16, fp16, i32 = mybir.dt.float32, mybir.dt.bfloat16, mybir.dt.float16, mybir.dt.int32
    u32 = mybir.dt.uint32
    ALU = mybir.AluOpType
    ACT = mybir.ActivationFunctionType
    AX = mybir.AxisListType

    ctx = ExitStack()
    with ctx:
        def sb(name, shape, dt):
            return ctx.enter_context(nc.sbuf_tensor(name, shape, dt))

        def sem(name):
            return ctx.enter_context(nc.semaphore(name))

        ids_s = sb("ids_s", [P, TILES, NF], i32)
        ids_f = sb("ids_f", [NL, BATCH], i32)
        field_c = sb("field_c", [NL, 2], fp32)
        part_c = sb("part_c", [P, 12], fp32)
        pow2 = sb("pow2", [P, 7], i32)
        onehot_w = sb("onehot_w", [QK, NG + 1, P], fp16)
        select_w = sb("select_w", [SK, 2, KC * P], bf16)
        ident = sb("ident", [P, P], fp32)
        rows = sb("rows", [P, RING, R * DIM], fp32)
        mrows = sb("mrows", [MQ, MR * DIM], fp32)
        sums = sb("sums", [P, NG * R + MR], fp32)
        rest = sb("rest", [P, NG * R + MR], fp32)
        sum_parts = sb("sum_parts", [P, PARTS, NG * R + MR], bf16)
        blocks = sb("blocks", [P, PARTS, NG, P], bf16)
        quot = sb("quot", [QK, BATCH], fp16)
        hot = sb("hot", [P, NG + 1, BATCH], bf16)
        mquot = sb("mquot", [P, 2, TILES], fp32)
        mlow = sb("mlow", [P, TILES], i32)
        bits = sb("bits", [P, NS, 5], i32)
        mbits = sb("mbits", [P, 7], i32)
        index = sb("index", [P, SLOTS, TPC, NGAT], i32)
        grows = sb("grows", [P, SLOTS, TPC, NGAT, DIM], fp32)
        s_all = sb("s_all", [P, TPC, PARTS, NF], fp32)
        gsums = sb("gsums", [P, TPC, NGAT], fp32)
        cut_a = sb("cut_a", [SK, CHUNK], bf16)
        rest_a = sb("rest_a", [SK, CHUNK], fp32)
        cut_b = sb("cut_b", [SK, CHUNK], bf16)
        s_parts = sb("s_parts", [SK, CHUNK], bf16)
        rowv = sb("rowv", [P, 2, CHUNK], fp32)
        z = sb("z", [P, KC - 1, CHUNK], fp32)
        zlast = sb("zlast", [LAST_K, BATCH], fp32)
        w1_s = sb("w1_s", [P, KC, H1], fp32)
        w2_s = sb("w2_s", [P, H1 // P, H2], fp32)
        w3_s = sb("w3_s", [P, H2 // P], fp32)
        b1_s = sb("b1_s", [P, H1 // P], fp32)
        b2_s = sb("b2_s", [P, H2 // P], fp32)
        h1_s = sb("h1_s", [P, H1 // P, CHUNK], fp32)
        h2_s = sb("h2_s", [P, H2 // P, CHUNK], fp32)
        y_s = sb("y_s", [1, CHUNK], fp32)

        ps = ctx.enter_context(nc.psum_tensor("ps", [P, 8, 512], fp32))
        X = ps[:, 0:2, :].rearrange("p b n -> p (b n)")
        B_H1, B_ROW, B_COL, B_SUM, B_H2 = 2, 4, 5, 6, 7

        def h1_ps(m):
            return ps[:, B_H1 + m // 2, m % 2 * CHUNK:(m % 2 + 1) * CHUNK]

        ld_ids = sem("ld_ids")
        ld_ids_s = sem("ld_ids_s")
        ld_field = sem("ld_field")
        ld_part = sem("ld_part")
        ld_pow2 = sem("ld_pow2")
        ld_onehot = sem("ld_onehot")
        ld_select = sem("ld_select")
        ld_ident = sem("ld_ident")
        ld_rows = [sem(f"ld_rows{g}") for g in range(NG)]
        ld_mrows = [sem(f"ld_mrows{i}") for i in range(2)]
        ld_w = sem("ld_w")
        ld_dense = sem("ld_dense")
        quot_clear = sem("quot_clear")
        sums_clear = sem("sums_clear")
        prep = sem("prep")
        quot_ready = sem("quot_ready")
        bcast_ready = sem("bcast_ready")
        hot_ready = sem("hot_ready")
        mhot_ready = sem("mhot_ready")
        blocks_ready = sem("blocks_ready")
        looked_mm = sem("looked_mm")
        bits_ready = sem("bits_ready")
        small_step = sem("small_step")
        medium_step = sem("medium_step")
        picked = sem("picked")
        index_ready = sem("index_ready")
        gathered_in = [sem(f"gathered_in{s}") for s in range(SLOTS)]
        grows_used = [sem(f"grows_used{s}") for s in range(SLOTS)]
        rows_used = sem("rows_used")
        sums_in = sem("sums_in")
        st_ready = sem("st_ready")
        cut_a_ready = sem("cut_a_ready")
        rest_a_ready = sem("rest_a_ready")
        cut_b_ready = sem("cut_b_ready")
        parts_ready = sem("parts_ready")
        select_ready = sem("select_ready")
        rowv_ready = sem("rowv_ready")
        z_ready = sem("z_ready")
        h1_ready = sem("h1_ready")
        h1_relu = sem("h1_relu")
        h2_ready = sem("h2_ready")
        h2_relu = sem("h2_relu")
        y_ready = sem("y_ready")
        y_copied = sem("y_copied")
        y_stored = sem("y_stored")

        NW = 7
        QB = BATCH // 512
        M1, M2 = H1 // P, H2 // P
        NZ = (KC + 1) // 2

        block = ctx.enter_context(nc.Block())


        @block.sync
        def _(sp):
            nc.sync.sem_inc(y_stored, 16)
            sp.dma_start(ids_f[:, :], ids_field).then_inc(ld_ids, 16)
            sp.dma_start(field_c[:, :], c_field).then_inc(ld_field, 16)
            sp.dma_start(onehot_w[:, :, :], c_onehot).then_inc(ld_onehot, 16)
            sp.dma_start(part_c[:, :], c_part).then_inc(ld_part, 16)

            def load_group(g):
                q, n, first, used = GROUPS[g]
                at = (first - len(A_FIELDS)) * q
                src = rows_a[g, :, :] if g < NGA else rows_b[at:at + used, :]
                if g >= RING:
                    sp.wait_ge(rows_used, g - RING + 1)
                sp.dma_start(rows[0:used, g % RING, :], src).then_inc(ld_rows[g], 16)

            for g in range(RING):
                load_group(g)
            half = MR // 2 * DIM
            for i in range(2):
                sp.dma_start(mrows[:, i * half:(i + 1) * half],
                             medium[:, i * half:(i + 1) * half]).then_inc(ld_mrows[i], 16)
            for g in range(RING, NG):
                load_group(g)
            sp.dma_start(ident[:, :], c_ident).then_inc(ld_ident, 16)
            sp.dma_start(select_w[:, :, :], c_select).then_inc(ld_select, 16)
            sp.dma_start(zlast[LAST_PAIRS:LAST_K, :], dense_t).then_inc(ld_w, 16)
            sp.dma_start(b1_s[:, :], b1).then_inc(ld_w, 16)
            sp.dma_start(b2_s[:, :], b2).then_inc(ld_w, 16)
            sp.dma_start(w3_s[:, :], w3).then_inc(ld_w, 16)
            sp.dma_start(w1_s[:, 0:KC - 1, :],
                         w1[0:(KC - 1) * P, :].rearrange("(c p) n -> p c n", p=P)).then_inc(ld_w, 16)
            sp.dma_start(w1_s[0:LAST_K, KC - 1, :], w1[(KC - 1) * P:NPAIR + NDENSE, :]).then_inc(ld_w, 16)
            sp.dma_start(w2_s[:, :, :], w2.rearrange("(c p) n -> p c n", p=P)).then_inc(ld_w, 16)
            with nc.sync.Fori(0, CHUNKS) as c:
                sp.wait_ge(y_copied, c + 1)
                sp.dma_start(y_out[:, bass.ds(c * CHUNK, CHUNK)], y_s[:, :]).then_inc(y_stored, 16)
            sp.wait_ge(y_stored, 16 * CHUNKS + 16)

        @block.gpsimd
        def _(pool):
            pool.wait_ge(ld_ids_s, 16)
            with nc.gpsimd.Fori(0, CHUNKS // SLOTS) as it:
                for s in range(SLOTS):
                    pool.wait_ge(grows_used[s], it + 1)
                    nc.gpsimd.tensor_copy(
                        index[:, s, :, :], ids_s[:, bass.ds(it * (SLOTS * TPC) + s * TPC, TPC), NL:NF]
                    ).then_inc(index_ready, 1)
                    pool.wait_ge(index_ready, s + 1)
                    for t in range(TPC):
                        for j in range(NGAT):
                            nc.gpsimd.indirect_dma_start(
                                out=grows[:, s, t, j, :], out_offset=None, in_=gathered[j],
                                in_offset=bass.IndirectOffsetOnAxis(ap=index[:, s, t, j:j + 1].bitcast(u32), axis=0),
                            ).then_inc(gathered_in[s], 16)
                nc.gpsimd.sem_clear(index_ready)

        @block.scalar
        def _(act):
            nc.scalar.sem_inc(hot_ready, 1)
            act.dma_start(ids_s[:, :, :], ids_sample).then_inc(ld_ids_s, 16)
            act.dma_start(pow2[:, :], c_pow2).then_inc(ld_pow2, 16)
            act.wait_ge(ld_part, 16)
            with nc.scalar.Fori(0, QB) as b:
                for g, (q, n, first, used) in enumerate(GROUPS):
                    act.wait_ge(bcast_ready, b * (NG + 1) + g + 1)
                    nc.scalar.activation(hot[0:used, g, bass.ds(b * 512, 512)], ps[0:used, g % 7, :], ACT.Relu,
                                         bias=part_c[0:used, 10:11] if g < NGA else part_c[0:used, 11:12]
                                         ).then_inc(hot_ready, 1)
            act.wait_ge(ld_w, 16 * NW)

            def cut(c):
                act.wait_ge(st_ready, c + 1)
                nc.scalar.activation(cut_a[:, :], ps[0:SK, B_SUM, 0:CHUNK], ACT.Copy).then_inc(cut_a_ready, 1)
                act.wait_ge(rest_a_ready, c + 1)
                nc.scalar.activation(cut_b[:, :], rest_a[:, :], ACT.Copy).then_inc(cut_b_ready, 1)

            def row_factor(c, k):
                act.wait_ge(select_ready, c * NZ + k + 1)
                if k < NZ - 1:
                    nc.scalar.activation(rowv[:, :, :], ps[:, B_ROW, :].rearrange("p (a n) -> p a n", a=2),
                                         ACT.Copy).then_inc(rowv_ready, 1)
                else:
                    nc.scalar.activation(rowv[:, 0, :], ps[:, B_ROW, 0:CHUNK], ACT.Copy)
                    nc.scalar.activation(rowv[0:LAST_PAIRS, 1, :], ps[0:LAST_PAIRS, B_ROW, CHUNK:],
                                         ACT.Copy).then_inc(rowv_ready, 1)

            def layers(c, last):
                row_factor(c, 1)
                row_factor(c, 2)
                for m in range(M1):
                    if m % 2 == 0:
                        act.wait_ge(h1_ready, c * (M1 // 2) + m // 2 + 1)
                    nc.scalar.activation(h1_s[:, m, :], h1_ps(m), ACT.Relu, bias=b1_s[:, m:m + 1]).then_inc(h1_relu, 1)
                if not last:
                    cut(c + 1)
                act.wait_ge(h2_ready, c + 1)
                for m in range(M2):
                    nc.scalar.activation(h2_s[:, m, :], ps[:, B_H2, m * CHUNK:(m + 1) * CHUNK], ACT.Relu,
                                         bias=b2_s[:, m:m + 1]).then_inc(h2_relu, 1)
                if not last:
                    row_factor(c + 1, 0)
                act.wait_ge(y_ready, c + 1)
                act.wait_ge(y_stored, (c + 1) * 16)
                nc.scalar.activation(y_s[:, :], ps[0:1, B_SUM, CHUNK:2 * CHUNK], ACT.Copy).then_inc(y_copied, 1)

            cut(0)
            row_factor(0, 0)
            with nc.scalar.Fori(0, CHUNKS - 1) as c:
                layers(c, False)
            layers(CHUNKS - 1, True)

        @block.vector
        def _(dve):
            chain = [0]

            def link(ins):
                chain[0] += 1
                ins.then_inc(prep, 1)
                dve.wait_ge(prep, chain[0])

            nc.vector.sem_inc(mhot_ready, 1)
            for s in range(SLOTS):
                nc.vector.sem_inc(grows_used[s], 1)
            nc.vector.memset(quot[:, :].bitcast(fp32), 0.0).then_inc(quot_clear, 1)
            nc.vector.memset(sums[:, :], 0.0).then_inc(sums_clear, 1)
            dve.wait_ge(quot_clear, 1)
            dve.wait_ge(ld_ids, 16)
            dve.wait_ge(ld_field, 16)
            link(nc.vector.tensor_scalar(ids_f[:, :].bitcast(fp32), ids_f[:, :], field_c[:, 0:1], field_c[:, 1:2],
                                         ALU.subtract, ALU.mult))
            link(nc.vector.tensor_scalar(quot[0:NL, :], ids_f[:, :].bitcast(fp32), ROUND, ROUND, ALU.add, ALU.subtract))
            nc.vector.tensor_tensor(quot[64:QK, :], quot[0:NS, :], quot[0:NS, :], ALU.mult).then_inc(quot_ready, 1)
            dve.wait_ge(ld_part, 16)

            def one_hot_medium(b):
                dve.wait_ge(bcast_ready, (b + 1) * (NG + 1))
                nc.vector.tensor_scalar(hot[0:MQ, NG, b * 512:(b + 1) * 512], ps[0:MQ, 7, :], part_c[0:MQ, 0:1],
                                        None, ALU.is_equal).then_inc(mhot_ready, 1)

            def sum_group(g):
                used = GROUPS[g][3]
                dve.wait_ge(ld_rows[g], 16)
                nc.vector.tensor_reduce(sums[0:used, g * R:(g + 1) * R],
                                        rows[0:used, g % RING, :].rearrange("p (r d) -> p r d", d=DIM), AX.X,
                                        ALU.add).then_inc(rows_used, 1)

            dve.wait_ge(sums_clear, 1)
            for g in range(RING):
                sum_group(g)
                if g:
                    one_hot_medium(g - 1)
            dve.wait_ge(ld_ids_s, 16)
            mid = ids_s[:, :, NS]
            link(nc.vector.tensor_scalar(mquot[:, 0, :], mid, (MR - 1) / 2, 1.0 / MR, ALU.subtract, ALU.mult))
            link(nc.vector.tensor_scalar(mquot[:, 1, :], mquot[:, 0, :], ROUND, ROUND, ALU.add, ALU.subtract))
            link(nc.vector.scalar_tensor_tensor(out=mlow[:, :], in0=mquot[:, 1, :], scalar=-float(MR), in1=mid,
                                                op0=ALU.mult, op1=ALU.add))
            for i in range(2):
                dve.wait_ge(ld_mrows[i], 16)
                h = MR // 2
                nc.vector.tensor_reduce(
                    sums[0:MQ, NG * R + i * h:NG * R + (i + 1) * h],
                    mrows[:, i * h * DIM:(i + 1) * h * DIM].rearrange("p (r d) -> p r d", d=DIM), AX.X,
                    ALU.add)
            for g in range(RING, NG):
                sum_group(g)
                if g == RING:
                    one_hot_medium(3)
            dve.wait_ge(rows_used, NG)
            link(nc.vector.tensor_copy(sum_parts[:, 0, :], sums[:, :]))
            link(nc.vector.tensor_tensor(rest[:, :], sums[:, :], sum_parts[:, 0, :], ALU.subtract))
            link(nc.vector.tensor_copy(sum_parts[:, 1, :], rest[:, :]))
            link(nc.vector.tensor_tensor(sum_parts[:, 2, :], rest[:, :], sum_parts[:, 1, :], ALU.subtract))
            small = sum_parts[:, :, 0:NG * R].rearrange("p a (g r) -> p a g r", r=R)
            for f in range(4):
                nc.vector.tensor_scalar(blocks[:, :, 0:NGA, f * R:(f + 1) * R], small[:, :, 0:NGA, :],
                                        part_c[:, 1 + f:2 + f], None, ALU.mult)
            for f in range(3):
                ins = nc.vector.tensor_scalar(blocks[:, :, NGA:NG, f * R:(f + 1) * R], small[:, :, NGA:NG, :],
                                              part_c[:, 5 + f:6 + f], None, ALU.mult)
            ins.then_inc(blocks_ready, 1)
            dve.wait_ge(ld_pow2, 16)
            x_small = X[:, 0:NS * R].rearrange("p (f r) -> p f r", r=R)
            x_mid = X[:, NS * R:NS * R + MR]

            def pick(c, t):
                tile = c * TPC + t
                nc.vector.tensor_tensor(
                    bits[:, :, :], ids_s[:, bass.ds(tile, 1), 0:NS].rearrange("p t f -> p (t f)").unsqueeze(2).broadcast_to([P, NS, 5]),
                    pow2[:, 0:5].unsqueeze(1).broadcast_to([P, NS, 5]), ALU.bitwise_and).then_inc(bits_ready, 1)
                dve.wait_ge(looked_mm, tile + 1)
                nc.vector.tensor_tensor(mbits[:, :], mlow[:, bass.ds(tile, 1)].broadcast_to([P, 7]), pow2[:, :],
                                        ALU.bitwise_and).then_inc(bits_ready, 1)
                dve.wait_ge(bits_ready, 2)
                for step in range(7):
                    k = 64 >> step
                    n = min(k, MR - k)
                    if step > 0:
                        dve.wait_ge(medium_step, step)
                    nc.vector.copy_predicated(x_mid[:, 0:n], mbits[:, 6 - step:7 - step].broadcast_to([P, n]),
                                              x_mid[:, k:k + n]).then_inc(medium_step, 1)
                    if step < 5:
                        k = 16 >> step
                        if step > 0:
                            dve.wait_ge(small_step, step)
                        nc.vector.copy_predicated(
                            x_small[:, :, 0:k], bits[:, :, 4 - step:5 - step].broadcast_to([P, NS, k]),
                            x_small[:, :, k:2 * k]).then_inc(small_step, 1)
                dve.wait_ge(small_step, 5)
                nc.vector.tensor_copy(s_all[:, t, :, 0:NS], x_small[:, :, 0].unsqueeze(1).broadcast_to([P, PARTS, NS]))
                dve.wait_ge(medium_step, 7)
                nc.vector.tensor_copy(s_all[:, t, :, NS:NL], x_mid[:, 0:1].unsqueeze(1).broadcast_to([P, PARTS, 1])).then_inc(picked, 1)
                for step_sem in (bits_ready, small_step, medium_step):
                    nc.vector.sem_clear(step_sem)

            def sum_gathered(s, it):
                dve.wait_ge(gathered_in[s], (it + 1) * (16 * TPC * NGAT))
                nc.vector.tensor_reduce(gsums[:, :, :], grows[:, s, :, :, :], AX.X,
                                        ALU.add).then_inc(grows_used[s], 1)
                dve.wait_ge(grows_used[s], it + 2)
                nc.vector.tensor_copy(s_all[:, :, :, NL:NF],
                                      gsums[:, :, :].unsqueeze(2).broadcast_to([P, TPC, PARTS, NGAT])
                                      ).then_inc(sums_in, 1)

            def cut(c):
                dve.wait_ge(cut_a_ready, c + 1)
                nc.vector.scalar_tensor_tensor(out=rest_a[:, :], in0=cut_a[:, :], scalar=part_c[0:SK, 8:9],
                                               in1=ps[0:SK, B_SUM, 0:CHUNK], op0=ALU.mult,
                                               op1=ALU.add).then_inc(rest_a_ready, 1)
                dve.wait_ge(cut_b_ready, c + 1)
                nc.vector.scalar_tensor_tensor(out=s_parts[:, :], in0=cut_b[:, :], scalar=part_c[0:SK, 9:10],
                                               in1=rest_a[:, :], op0=ALU.mult, op1=ALU.add).then_inc(parts_ready, 1)

            def products(c, k):
                dve.wait_ge(rowv_ready, c * NZ + k + 1)
                if k < NZ - 1:
                    nc.vector.tensor_tensor(z[:, 2 * k:2 * k + 2, :], rowv[:, :, :],
                                            ps[:, B_COL, :].rearrange("p (a n) -> p a n", a=2),
                                            ALU.mult).then_inc(z_ready, 1)
                else:
                    nc.vector.tensor_tensor(z[:, 2 * k, :], rowv[:, 0, :], ps[:, B_COL, 0:CHUNK], ALU.mult)
                    nc.vector.tensor_tensor(zlast[0:LAST_PAIRS, bass.ds(c * CHUNK, CHUNK)], rowv[0:LAST_PAIRS, 1, :],
                                            ps[0:LAST_PAIRS, B_COL, CHUNK:], ALU.mult).then_inc(z_ready, 1)

            def step(c, s_next, it_next):
                products(c, 1)
                if s_next is not None:
                    pick(c + 1, 0)
                products(c, 2)
                if s_next is not None:
                    pick(c + 1, 1)
                    sum_gathered(s_next, it_next)
                    cut(c + 1)
                    products(c + 1, 0)

            pick(0, 0)
            pick(0, 1)
            sum_gathered(0, 0)
            cut(0)
            dve.wait_ge(ld_w, 16 * NW)
            products(0, 0)
            with nc.vector.Fori(0, CHUNKS // SLOTS - 1) as it:
                for s in range(SLOTS):
                    step(it * SLOTS + s, (s + 1) % SLOTS, it + (s + 1) // SLOTS)
            step(CHUNKS - 2, SLOTS - 1, CHUNKS // SLOTS - 1)
            step(CHUNKS - 1, None, None)

        @block.tensor
        def _(pe):
            pe.wait_ge(ld_onehot, 16)
            pe.wait_ge(quot_ready, 1)
            with nc.tensor.Fori(0, QB) as b:
                for g, (q, n, first, used) in enumerate(GROUPS):
                    if g == 0:
                        pe.wait_ge(hot_ready, b * NG + 1)
                    elif g >= 7:
                        pe.wait_ge(hot_ready, b * NG + g - 5)
                    nc.tensor.matmul(ps[0:used, g % 7, :], onehot_w[:, g, 0:used], quot[:, bass.ds(b * 512, 512)],
                                     start=True, stop=True).then_inc(bcast_ready, 1)
                pe.wait_ge(mhot_ready, b + 1)
                nc.tensor.matmul(ps[0:MQ, 7, :], onehot_w[:, NG, 0:MQ], quot[:, bass.ds(b * 512, 512)],
                                 start=True, stop=True).then_inc(bcast_ready, 1)
            pe.wait_ge(blocks_ready, 1)
            pe.wait_ge(hot_ready, QB * NG + 1)
            pe.wait_ge(mhot_ready, QB + 1)

            def look_up(c, t):
                tile = c * TPC + t
                at = tile * P
                for g, (q, n, first, used) in enumerate(GROUPS):
                    for a in range(PARTS):
                        nc.tensor.matmul(X[:, first * R:(first + n) * R], hot[0:used, g, bass.ds(at, P)],
                                         blocks[0:used, a, g, 0:n * R], start=a == 0, stop=a == PARTS - 1)
                for a in range(PARTS):
                    ins = nc.tensor.matmul(X[:, NS * R:NS * R + MR], hot[0:MQ, NG, bass.ds(at, P)],
                                           sum_parts[0:MQ, a, NG * R:], start=a == 0, stop=a == PARTS - 1)
                ins.then_inc(looked_mm, 1)

            def transpose_sums(c):
                pe.wait_ge(picked, (c + 1) * TPC)
                pe.wait_ge(sums_in, c + 1)
                for t in range(TPC):
                    ins = nc.tensor.matmul(ps[0:SK, B_SUM, t * P:(t + 1) * P],
                                           s_all[:, t, :, :].rearrange("p a f -> p (a f)"), ident[:, :],
                                           start=True, stop=True)
                ins.then_inc(st_ready, 1)

            def select(c, k):
                if k == 0:
                    pe.wait_ge(parts_ready, c + 1)
                else:
                    pe.wait_ge(z_ready, c * NZ + k)
                for side, bank in ((0, B_ROW), (1, B_COL)):
                    for a in range(2):
                        kc = 2 * k + a
                        m = P if kc < KC - 1 else LAST_PAIRS
                        ins = nc.tensor.matmul(ps[0:m, bank, a * CHUNK:(a + 1) * CHUNK],
                                               select_w[:, side, kc * P:kc * P + m], s_parts[:, :],
                                               start=True, stop=True)
                ins.then_inc(select_ready, 1)

            def layer1(c, k):
                pe.wait_ge(z_ready, c * NZ + k + 1)
                for kc in (2 * k, 2 * k + 1):
                    for m in range(M1):
                        if kc < KC - 1:
                            nc.tensor.matmul(h1_ps(m), w1_s[:, kc, m * P:(m + 1) * P], z[:, kc, :],
                                             start=kc == 0 and m % 2 == 0, stop=False, skip_group_check=True)
                        else:
                            ins = nc.tensor.matmul(h1_ps(m), w1_s[0:LAST_K, kc, m * P:(m + 1) * P],
                                                   zlast[:, bass.ds(c * CHUNK, CHUNK)], start=False, stop=True,
                                                   skip_group_check=True)
                            if m % 2:
                                ins.then_inc(h1_ready, 1)

            def layer2(c):
                for m in range(M2):
                    for k in range(M1):
                        if m == 0:
                            pe.wait_ge(h1_relu, c * M1 + k + 1)
                        ins = nc.tensor.matmul(ps[:, B_H2, m * CHUNK:(m + 1) * CHUNK], w2_s[:, k, m * P:(m + 1) * P],
                                               h1_s[:, k, :], start=k == 0, stop=k == M1 - 1)
                ins.then_inc(h2_ready, 1)

            def layer3(c):
                for k in range(M2):
                    pe.wait_ge(h2_relu, c * M2 + k + 1)
                    ins = nc.tensor.matmul(ps[0:1, B_SUM, CHUNK:2 * CHUNK], w3_s[:, k:k + 1], h2_s[:, k, :],
                                           start=k == 0, stop=k == M2 - 1)
                ins.then_inc(y_ready, 1)

            def step(c, last):
                select(c, 1)
                layer1(c, 0)
                if not last:
                    look_up(c + 1, 0)
                select(c, 2)
                layer1(c, 1)
                if not last:
                    pe.wait_ge(picked, (c + 1) * TPC + 1)
                    look_up(c + 1, 1)
                layer1(c, 2)
                if not last:
                    transpose_sums(c + 1)
                layer2(c)
                if not last:
                    select(c + 1, 0)
                layer3(c)

            look_up(0, 0)
            pe.wait_ge(picked, 1)
            look_up(0, 1)
            pe.wait_ge(ld_ident, 16)
            transpose_sums(0)
            pe.wait_ge(ld_select, 16)
            select(0, 0)
            pe.wait_ge(ld_w, 16 * NW)
            with nc.tensor.Fori(0, CHUNKS - 1) as c:
                step(c, False)
            step(CHUNKS - 1, True)


def kernel(**inputs):
    import numpy as np
    import ml_dtypes
    import concourse.bacc as bacc
    from concourse.bass_utils import run_bass_kernel_spmd

    f32 = np.float32
    arrays = {}
    ids = np.ascontiguousarray(inputs["ids"])[:, ORDER]
    arrays["ids_sample"] = np.ascontiguousarray(ids.reshape(TILES, P, NF).transpose(1, 0, 2))
    arrays["ids_field"] = np.ascontiguousarray(ids[:, :NL].T)

    def filled(f, rows):
        table = np.asarray(inputs[f"tbl_{f}"])
        return np.concatenate([table, table[:rows - table.shape[0]]]).reshape(-1, R * DIM)

    arrays["rows_a"] = np.concatenate([filled(f, 32 * R) for f in A_FIELDS]).reshape(NGA, P, R * DIM)
    arrays["rows_b"] = np.concatenate([filled(f, 40 * R) for f in B_FIELDS])
    arrays["medium"] = np.asarray(inputs[f"tbl_{DENSE_MEDIUM[0]}"]).reshape(MQ, MR * DIM)
    for j, f in enumerate(GATHERED):
        arrays[f"gathered_{j}"] = np.asarray(inputs[f"tbl_{f}"])
    arrays["dense_t"] = np.ascontiguousarray(np.asarray(inputs["dense_ctx"]).T)
    arrays["w1"] = np.asarray(inputs["W_top1"])
    arrays["b1"] = np.ascontiguousarray(np.asarray(inputs["b_top1"]).reshape(H1 // P, P).T)
    arrays["w2"] = np.asarray(inputs["W_top2"])
    arrays["b2"] = np.ascontiguousarray(np.asarray(inputs["b_top2"]).reshape(H2 // P, P).T)
    arrays["w3"] = np.ascontiguousarray(np.asarray(inputs["W_top3"]).reshape(H2 // P, P).T)

    c_field = np.zeros((NL, 2), f32)
    c_field[:, 0], c_field[:, 1] = (R - 1) / 2, 1 / R
    c_field[NS:, 0], c_field[NS:, 1] = (MR - 1) / 2, 1 / MR
    part = np.arange(P)
    c_part = np.zeros((P, 12), f32)
    c_part[:, 0] = part
    for k in range(4):
        c_part[:, 1 + k] = part // 32 == k
    for k in range(3):
        c_part[:, 5 + k] = part // 40 == k
    c_part[:, 8] = -1.0 * (part >= NF)
    c_part[:, 9] = -1.0 * (part >= 2 * NF)
    c_part[:, 10] = 1 - (part % 32) ** 2
    c_part[:, 11] = 1 - (part % 40) ** 2
    c_pow2 = np.tile(2 ** np.arange(7, dtype=np.int32), (P, 1)).astype(np.int32)
    c_onehot = np.zeros((QK, NG + 1, P), np.float16)
    for g, (q, n, first, used) in enumerate(GROUPS):
        for p in range(used):
            h = p % q
            c_onehot[first + p // q, g, p] = 2 * h
            c_onehot[64 + first + p // q, g, p] = -1
    c_onehot[NS, NG, :] = 1
    c_select = np.zeros((PARTS, NF, 2, KC * P), f32)
    rows, cols = np.triu_indices(NF, k=1)
    for n, (i, j) in enumerate(zip(rows, cols)):
        c_select[:, POS[i], 0, n] = 1
        c_select[:, POS[j], 1, n] = 1
    arrays["c_field"], arrays["c_part"], arrays["c_pow2"], arrays["c_onehot"] = c_field, c_part, c_pow2, c_onehot
    arrays["c_select"] = c_select.reshape(SK, 2, KC * P).astype(ml_dtypes.bfloat16)
    arrays["c_ident"] = np.eye(P, dtype=f32)

    nc = bacc.Bacc("TRN2", target_bir_lowering=False, num_devices=1)
    ap = {n: nc.dram_tensor(n, a.shape, mybir.dt.from_np(a.dtype), kind="ExternalInput").ap() for n, a in arrays.items()}
    y = nc.dram_tensor("y_out", (1, BATCH), mybir.dt.float32, kind="ExternalOutput").ap()
    tower(nc, ap["ids_sample"], ap["ids_field"], ap["rows_a"], ap["rows_b"], ap["medium"],
          [ap[f"gathered_{j}"] for j in range(NGAT)], ap["dense_t"], ap["w1"], ap["b1"], ap["w2"], ap["b2"],
          ap["w3"], ap["c_field"], ap["c_part"], ap["c_pow2"], ap["c_onehot"], ap["c_select"], ap["c_ident"], y)
    r = run_bass_kernel_spmd(nc, [arrays], core_ids=[0])
    return r.results[0]["y_out"].reshape(BATCH, 1)
```

```python
import concourse.bass as bass
from concourse import mybir
from contextlib import ExitStack

VOCABS = [1000, 12500, 125000, 12500, 1000, 1250, 1250, 125000, 1250, 12500, 125000, 1000, 12500,
          12500, 12500, 1000, 1250, 1000, 1000, 12500, 1000, 1000, 12500, 1000, 1000, 1250, 1000,
          1250, 1000, 1250, 1000, 1000, 1000, 1000, 1250, 1000, 1000, 1000, 1000]
BATCH = 2048
DIM = 64
P = 128
NF = len(VOCABS)
NPAIR = NF * (NF - 1) // 2
NDENSE = 16
H1, H2 = 512, 256

R = 32
Q_A, FPG_A = 32, 4
Q_B, FPG_B = 40, 3
A_FIELDS = [f for f, v in enumerate(VOCABS) if v == 1000]
B_FIELDS = [f for f, v in enumerate(VOCABS) if v == 1250]
SMALL = A_FIELDS + B_FIELDS
NS = len(SMALL)
GROUPS = []
for fields, q, fpg in ((A_FIELDS, Q_A, FPG_A), (B_FIELDS, Q_B, FPG_B)):
    for start in range(0, len(fields), fpg):
        n = min(fpg, len(fields) - start)
        GROUPS.append((q, n, SMALL.index(fields[start]), n * q))
NG = len(GROUPS)
NGA = sum(g[0] == Q_A for g in GROUPS)
NG_FIRST = NGA - 1
MEDIUM = [f for f, v in enumerate(VOCABS) if v == 12500]
MR, MQ = 100, 125
NM = 1
MPITCH = 128
DENSE_MEDIUM = MEDIUM[:NM]
GATHERED = MEDIUM[NM:] + [f for f, v in enumerate(VOCABS) if v == 125000]
NGAT = len(GATHERED)
ORDER = SMALL + DENSE_MEDIUM + GATHERED
NL = NS + NM
LATE_STEPS = 4
POS = {f: i for i, f in enumerate(ORDER)}
PAIRS = [(i, j) for i in range(NF) for j in range(i + 1, NF)]

TILES = BATCH // P
CHUNK = 256
TPC = CHUNK // P
CHUNKS = BATCH // CHUNK
SLOTS = 2
ROUNDS = CHUNKS // SLOTS
RING = 4
KC = (NPAIR + NDENSE + P - 1) // P
LAST_PAIRS = NPAIR - (KC - 1) * P
LAST_K = LAST_PAIRS + NDENSE + 1
PARTS = 3
QK = 64 + NS
SK = PARTS * NF
ROUND = 12582912.0
LATE_FROM = CHUNKS - LATE_STEPS
EARLY_ROUNDS = LATE_FROM // SLOTS
LATE_AT = NM * MR + NG * R
NCOL = LATE_AT + MR
LATE_PIECES = 5
LATE_R = MR // LATE_PIECES
NEG_PART, ONE, BIAS_A, BIAS_B, MASK_A, MASK_B = 0, 1, 2, 3, 4, 4 + FPG_A
NPART = MASK_B + FPG_B


def tower(nc, ids_sample, ids_gather, ids_field, rows_a, rows_b, medium, gathered, dense_t, w1, w2, b2, w3,
          c_field, c_part, c_pow2, c_onehot, c_select, c_ident, y_out):
    fp32, bf16, fp16 = mybir.dt.float32, mybir.dt.bfloat16, mybir.dt.float16
    fp32r, i32, u32 = mybir.dt.float32r, mybir.dt.int32, mybir.dt.uint32
    ALU = mybir.AluOpType
    ACT = mybir.ActivationFunctionType
    AX = mybir.AxisListType

    ctx = ExitStack()
    with ctx:
        def sb(name, shape, dt):
            return ctx.enter_context(nc.sbuf_tensor(name, shape, dt))

        def sem(name):
            return ctx.enter_context(nc.semaphore(name))

        ids_s = sb("ids_s", [P, TILES, NL + 1], i32)
        ids_g = sb("ids_g", [P, TILES, NGAT], i32)
        field_c = sb("field_c", [NL + 1, 2], fp32)
        part_c = sb("part_c", [P, NPART], fp32)
        pow2 = sb("pow2", [P, 7], i32)
        onehot_w = sb("onehot_w", [QK, NG + NM + 1, P], fp16)
        select_w = sb("select_w", [SK, 2, KC * P], bf16)
        ident = sb("ident", [P, P], bf16)
        rows = sb("rows", [P, RING, R * DIM], fp32)
        late_rows = rows.rearrange("p a b -> p (a b)")[0:MQ, 0:MR * DIM]
        stage = sb("stage", [P, MR * DIM], fp32)
        w1_raw = stage[:, 0:KC * H1].rearrange("p (c n) -> p c n", n=H1)
        w2_raw = stage[:, KC * H1:KC * H1 + H1 // P * H2].rearrange("p (c n) -> p c n", n=H2)
        sums = sb("sums", [P, NCOL], fp32)
        rest = sb("rest", [P, NCOL], fp32)
        sum_parts = sb("sum_parts", [P, PARTS, NCOL], bf16)
        blocks = sb("blocks", [P, PARTS, NG, P], bf16)
        quot = sb("quot", [QK, BATCH], fp16)
        hot = sb("hot", [P, NG + NM, BATCH], bf16)
        late_hot = sb("late_hot", [P, LATE_STEPS * CHUNK], bf16)
        ids_f = hot[0:NL + 1, NG + NM - 2:NG + NM, :].rearrange("p a b -> p (a b)").bitcast(i32)
        quot_raw = hot[0:NL + 1, NG + NM - 2:NG + NM, :].rearrange("p a b -> p (a b)").bitcast(fp32)
        mquot = sb("mquot", [P, 2, TILES, NM + 1], fp32)
        mlow = sb("mlow", [P, TILES, NM + 1], i32)
        bits = sb("bits", [P, TPC, NS, 5], i32)
        mbits = sb("mbits", [P, TPC, NM + 1, 7], i32)
        index = sb("index", [P, SLOTS, TPC, NGAT], i32)
        grows = sb("grows", [P, SLOTS, TPC, NGAT, DIM], fp32)
        s_raw = sb("s_raw", [P, SLOTS, TPC, NF], fp32)
        s_rest = sb("s_rest", [P, TPC, NF], fp32)
        s_cut = sb("s_cut", [P, TPC, PARTS, NF], bf16)
        s_parts = sb("s_parts", [SK, CHUNK], bf16)
        rowv = sb("rowv", [P, 2, CHUNK], fp32)
        z_raw = sb("z_raw", [P, 2, CHUNK], fp32)
        z_last = sb("z_last", [LAST_K, BATCH], fp32)
        z_hi = sb("z_hi", [P, KC, CHUNK], fp32r)
        z_lo = sb("z_lo", [P, KC, CHUNK], fp32r)
        w1_hi = sb("w1_hi", [P, KC, H1], fp32r)
        w1_lo = sb("w1_lo", [P, KC, H1], fp32r)
        w2_hi = sb("w2_hi", [P, H1 // P, H2], fp32r)
        w2_lo = sb("w2_lo", [P, H1 // P, H2], fp32r)
        w3_s = sb("w3_s", [P, H2 // P], fp32)
        b2_s = sb("b2_s", [P, H2 // P], fp32)
        h1_hi = sb("h1_hi", [P, H1 // P, CHUNK], fp32r)
        h1_lo = sb("h1_lo", [P, H1 // P, CHUNK], fp32r)
        h2_s = sb("h2_s", [P, H2 // P, CHUNK], fp32)
        y_s = sb("y_s", [P, TPC], fp32)

        ps = ctx.enter_context(nc.psum_tensor("ps", [P, 8, 512], fp32))
        X = ps[:, 0:3 * TPC, :].rearrange("p (t b) n -> p t (b n)", t=TPC)
        B_H1, B_ROW, B_COL, B_H2 = 3, 5, 6, 7
        B_Y = B_H2

        def halves(bank):
            return ps[:, bank, :].rearrange("p (a n) -> p a n", a=2)

        ld_ids = sem("ld_ids")
        ld_ids_s = sem("ld_ids_s")
        ld_ids_g = [sem(f"ld_ids_g{i}") for i in range(2)]
        ld_field = sem("ld_field")
        ld_part = sem("ld_part")
        ld_pow2 = sem("ld_pow2")
        ld_onehot = sem("ld_onehot")
        ld_select = sem("ld_select")
        ld_ident = sem("ld_ident")
        ld_rows = [sem(f"ld_rows{g}") for g in range(NG)]
        ld_middle = [sem(f"ld_middle{i}") for i in range(2)]
        ld_small_w = sem("ld_small_w")
        ld_w = sem("ld_w")
        ld_late = [sem(f"ld_late{i}") for i in range(LATE_PIECES)]
        quot_clear = sem("quot_clear")
        sums_clear = sem("sums_clear")
        prep = sem("prep")
        quot_ready = sem("quot_ready")
        bcast_ready = sem("bcast_ready")
        mbcast_ready = sem("mbcast_ready")
        hot_ready = sem("hot_ready")
        square_ready = sem("square_ready")
        mhot_ready = sem("mhot_ready")
        rows_used = sem("rows_used")
        middle_used = sem("middle_used")
        blocks_ready = sem("blocks_ready")
        late_pieces = sem("late_pieces")
        late_summed = sem("late_summed")
        late_cut = sem("late_cut")
        w_hi_ready = sem("w_hi_ready")
        w_lo_ready = sem("w_lo_ready")
        looked_mm = sem("looked_mm")
        bits_ready = sem("bits_ready")
        small_step = sem("small_step")
        middle_step = sem("middle_step")
        picked = sem("picked")
        index_ready = sem("index_ready")
        gathered_in = [sem(f"gathered_in{s}") for s in range(SLOTS)]
        grows_used = [sem(f"grows_used{s}") for s in range(SLOTS)]
        cut_step = sem("cut_step")
        cut_ready = sem("cut_ready")
        st_ready = sem("st_ready")
        parts_ready = sem("parts_ready")
        select_ready = sem("select_ready")
        rowv_ready = sem("rowv_ready")
        z_ready = sem("z_ready")
        z_hi_ready = sem("z_hi_ready")
        z_lo_ready = sem("z_lo_ready")
        h1_ready = sem("h1_ready")
        h1_hi_ready = sem("h1_hi_ready")
        h1_lo_ready = sem("h1_lo_ready")
        h2_ready = sem("h2_ready")
        h2_relu = sem("h2_relu")
        y_ready = sem("y_ready")
        y_copied = sem("y_copied")
        y_stored = sem("y_stored")

        QB = BATCH // 512
        LATE_QB = LATE_STEPS * CHUNK // 512
        M1, M2 = H1 // P, H2 // P
        NZ = (KC + 1) // 2
        NSW = 3
        NW = 3

        block = ctx.enter_context(nc.Block())


        @block.sync
        def _(sp):
            nc.sync.sem_inc(y_stored, 16)
            sp.dma_start(ids_g[:, 0:TPC, :], ids_gather[:, 0:TPC, :]).then_inc(ld_ids_g[0], 16)
            sp.dma_start(ids_f, ids_field).then_inc(ld_ids, 16)
            half = MR // 2 * DIM
            for m in range(NM):
                for i in range(2):
                    if m:
                        sp.wait_ge(middle_used, 2 * (m - 1) + i + 1)
                    sp.dma_start(stage[0:MQ, i * half:(i + 1) * half],
                                 medium[m, :, i * half:(i + 1) * half]).then_inc(ld_middle[i], 16)
            for g, (q, n, first, used) in enumerate(GROUPS):
                if g >= RING:
                    sp.wait_ge(rows_used, g - RING + 1)
                at = (first - len(A_FIELDS)) * q
                src = rows_a[g, :, :] if g < NGA else rows_b[at:at + used, :]
                sp.dma_start(rows[0:used, g % RING, :], src).then_inc(ld_rows[g], 16)
            sp.dma_start(ident[:, :], c_ident).then_inc(ld_ident, 16)
            sp.wait_ge(middle_used, 2 * NM)
            sp.dma_start(w1_raw[:, 0:KC - 1, :],
                         w1[0:(KC - 1) * P, :].rearrange("(c p) n -> p c n", p=P)).then_inc(ld_w, 16)
            sp.dma_start(w1_raw[0:LAST_K, KC - 1, :], w1[(KC - 1) * P:(KC - 1) * P + LAST_K, :]).then_inc(ld_w, 16)
            sp.dma_start(select_w[:, :, :], c_select).then_inc(ld_select, 16)
            sp.dma_start(w2_raw, w2.rearrange("(c p) n -> p c n", p=P)).then_inc(ld_w, 16)
            sp.dma_start(z_last[LAST_PAIRS:LAST_K, :], dense_t).then_inc(ld_small_w, 16)
            sp.dma_start(b2_s[:, :], b2).then_inc(ld_small_w, 16)
            sp.dma_start(w3_s[:, :], w3).then_inc(ld_small_w, 16)
            sp.wait_ge(rows_used, NG)
            late = gathered[0].rearrange("(q r) d -> q (r d)", q=MQ)
            for i in range(LATE_PIECES):
                at = slice(i * LATE_R * DIM, (i + 1) * LATE_R * DIM)
                sp.dma_start(late_rows[:, at], late[:, at]).then_inc(ld_late[i], 16)
            for i in range(LATE_PIECES):
                sp.wait_ge(ld_late[i], 16)
                nc.sync.sem_inc(late_pieces, 1)
            with nc.sync.Fori(0, CHUNKS) as c:
                sp.wait_ge(y_copied, c + 2)
                sp.dma_start(y_out[bass.ds(c, 1), :, :].rearrange("c p t -> p (c t)"), y_s[:, :]).then_inc(y_stored, 16)
            sp.wait_ge(y_stored, 16 * CHUNKS + 16)

        @block.gpsimd
        def _(pool):
            pool.wait_ge(ld_ids_g[0], 16)

            def gather(it, s, j0):
                if s > 0:
                    pool.wait_ge(ld_ids_g[1], 16)
                pool.wait_ge(grows_used[s], it + 1)
                nc.gpsimd.tensor_copy(
                    index[:, s, :, :], ids_g[:, bass.ds(it * (SLOTS * TPC) + s * TPC, TPC), :]
                ).then_inc(index_ready, 1)
                pool.wait_ge(index_ready, s + 1)
                for t in range(TPC):
                    for j in range(j0, NGAT):
                        nc.gpsimd.indirect_dma_start(
                            out=grows[:, s, t, j, :], out_offset=None, in_=gathered[j],
                            in_offset=bass.IndirectOffsetOnAxis(ap=index[:, s, t, j:j + 1].bitcast(u32), axis=0),
                        ).then_inc(gathered_in[s], 16)

            for lo, hi, j0 in ((0, EARLY_ROUNDS, 0), (EARLY_ROUNDS, ROUNDS, 1)):
                with nc.gpsimd.Fori(lo, hi) as it:
                    for s in range(SLOTS):
                        gather(it, s, j0)
                    nc.gpsimd.sem_clear(index_ready)

        @block.scalar
        def _(act):
            nc.scalar.sem_inc(hot_ready, NG)
            nc.scalar.sem_inc(y_copied, 1)
            act.dma_start(field_c[:, :], c_field).then_inc(ld_field, 16)
            act.dma_start(onehot_w[:, :, :], c_onehot).then_inc(ld_onehot, 16)
            act.dma_start(part_c[:, :], c_part).then_inc(ld_part, 16)
            act.dma_start(ids_s[:, :, :], ids_sample).then_inc(ld_ids_s, 16)
            act.dma_start(ids_g[:, TPC:TILES, :], ids_gather[:, TPC:TILES, :]).then_inc(ld_ids_g[1], 16)
            act.dma_start(pow2[:, :], c_pow2).then_inc(ld_pow2, 16)
            act.wait_ge(ld_part, 16)
            bias_a, bias_b = part_c[:, BIAS_A:BIAS_A + 1], part_c[:, BIAS_B:BIAS_B + 1]
            neg_part, one = part_c[0:MQ, NEG_PART:NEG_PART + 1], part_c[0:MQ, ONE:ONE + 1]
            with nc.scalar.Fori(0, QB) as b:
                for g, (q, n, first, used) in enumerate(GROUPS):
                    act.wait_ge(bcast_ready, b * NG + g + 1)
                    nc.scalar.activation(hot[0:used, g, bass.ds(b * 512, 512)], ps[0:used, g, :], ACT.Relu,
                                         bias=bias_a[0:used, :] if g < NGA else bias_b[0:used, :]
                                         ).then_inc(hot_ready, 1)

            def middle_one_hot(n, bank, to):
                act.wait_ge(mbcast_ready, n + 1)
                nc.scalar.activation(ps[0:MQ, bank, :], ps[0:MQ, bank, :], ACT.Square,
                                     bias=neg_part).then_inc(square_ready, 1)
                act.wait_ge(square_ready, n + 1)
                nc.scalar.activation(to, ps[0:MQ, bank, :], ACT.Relu, bias=one, scale=-1.0).then_inc(mhot_ready, 1)

            for m in range(NM):
                for b in range(QB):
                    middle_one_hot(m * QB + b, b, hot[0:MQ, NG + m, b * 512:(b + 1) * 512])
            for b in range(LATE_QB):
                middle_one_hot(NM * QB + b, QB + b, late_hot[0:MQ, b * 512:(b + 1) * 512])
            act.wait_ge(ld_w, 16 * NW)
            for k in range(NZ - 1):
                nc.scalar.activation(w1_hi[:, 2 * k:2 * k + 2, :], w1_raw[:, 2 * k:2 * k + 2, :],
                                     ACT.Copy).then_inc(w_hi_ready, 1)
            nc.scalar.activation(w1_hi[:, KC - 2, :], w1_raw[:, KC - 2, :], ACT.Copy)
            nc.scalar.activation(w1_hi[0:LAST_K, KC - 1, :], w1_raw[0:LAST_K, KC - 1, :],
                                 ACT.Copy).then_inc(w_hi_ready, 1)
            nc.scalar.activation(w2_hi[:, :, :], w2_raw, ACT.Copy).then_inc(w_hi_ready, 1)
            act.wait_ge(ld_small_w, 16 * NSW)

            def parts_by_field(c):
                act.wait_ge(st_ready, c + 1)
                nc.scalar.activation(s_parts[:, :], ps[0:SK, B_COL, 0:CHUNK], ACT.Copy).then_inc(parts_ready, 1)

            def row_factor(c, k):
                act.wait_ge(select_ready, c * NZ + k + 1)
                if k < NZ - 1:
                    nc.scalar.activation(rowv[:, :, :], halves(B_ROW), ACT.Copy).then_inc(rowv_ready, 1)
                else:
                    nc.scalar.activation(rowv[:, 0, :], ps[:, B_ROW, 0:CHUNK], ACT.Copy)
                    nc.scalar.activation(rowv[0:LAST_PAIRS, 1, :], ps[0:LAST_PAIRS, B_ROW, CHUNK:],
                                         ACT.Copy).then_inc(rowv_ready, 1)

            def round_products(c, k):
                act.wait_ge(z_ready, c * NZ + k + 1)
                if k < NZ - 1:
                    nc.scalar.activation(z_hi[:, 2 * k:2 * k + 2, :], z_raw[:, :, :], ACT.Copy).then_inc(z_hi_ready, 1)
                else:
                    nc.scalar.activation(z_hi[:, KC - 2, :], z_raw[:, 0, :], ACT.Copy)
                    nc.scalar.activation(z_hi[0:LAST_K, KC - 1, :], z_last[:, bass.ds(c * CHUNK, CHUNK)],
                                         ACT.Copy).then_inc(z_hi_ready, 1)

            def hidden1(c):
                for pair in range(M1 // 2):
                    act.wait_ge(h1_ready, c * (M1 // 2) + pair + 1)
                    nc.scalar.activation(h1_hi[:, 2 * pair:2 * pair + 2, :], halves(B_H1 + pair),
                                         ACT.Relu).then_inc(h1_hi_ready, 1)

            def hidden2(c):
                act.wait_ge(h2_ready, c + 1)
                for m in range(M2):
                    nc.scalar.activation(h2_s[:, m, :], ps[:, B_H2, m * CHUNK:(m + 1) * CHUNK], ACT.Relu,
                                         bias=b2_s[:, m:m + 1]).then_inc(h2_relu, 1)

            def result(c):
                act.wait_ge(y_ready, c + 1)
                act.wait_ge(y_stored, (c + 1) * 16)
                nc.scalar.activation(y_s[:, :], ps[:, B_Y, 0:TPC], ACT.Copy).then_inc(y_copied, 1)

            parts_by_field(0)
            for k in range(NZ):
                row_factor(0, k)
                round_products(0, k)

            def step(c, last):
                hidden1(c - 1)
                parts_by_field(c)
                row_factor(c, 0)
                round_products(c, 0)
                row_factor(c, 1)
                hidden2(c - 1)
                round_products(c, 1)
                if last:
                    row_factor(c, 2)
                    result(c - 1)
                else:
                    result(c - 1)
                    row_factor(c, 2)
                round_products(c, 2)

            with nc.scalar.Fori(1, CHUNKS - 1) as c:
                step(c, False)
            step(CHUNKS - 1, True)
            hidden1(CHUNKS - 1)
            hidden2(CHUNKS - 1)
            result(CHUNKS - 1)

        @block.vector
        def _(dve):
            chain = [0]

            def link(ins):
                chain[0] += 1
                ins.then_inc(prep, 1)
                dve.wait_ge(prep, chain[0])

            for s in range(SLOTS):
                nc.vector.sem_inc(grows_used[s], 1)
            nc.vector.memset(quot[:, :].bitcast(fp32), 0.0).then_inc(quot_clear, 1)
            nc.vector.memset(sums[:, :], 0.0).then_inc(sums_clear, 1)
            dve.wait_ge(quot_clear, 1)
            dve.wait_ge(ld_ids, 16)
            dve.wait_ge(ld_field, 16)
            link(nc.vector.tensor_scalar(quot_raw, ids_f, field_c[:, 0:1], field_c[:, 1:2], ALU.subtract, ALU.mult))
            link(nc.vector.tensor_scalar(quot[0:NL + 1, :], quot_raw, ROUND, ROUND, ALU.add, ALU.subtract))
            nc.vector.tensor_tensor(quot[64:QK, :], quot[0:NS, :], quot[0:NS, :], ALU.mult).then_inc(quot_ready, 1)
            dve.wait_ge(ld_part, 16)

            dve.wait_ge(sums_clear, 1)
            h = MR // 2
            for m in range(NM):
                for i in range(2):
                    dve.wait_ge(ld_middle[i], 16 * (m + 1))
                    nc.vector.tensor_reduce(
                        sums[0:MQ, m * MR + i * h:m * MR + (i + 1) * h],
                        stage[0:MQ, i * h * DIM:(i + 1) * h * DIM].rearrange("p (r d) -> p r d", d=DIM), AX.X,
                        ALU.add).then_inc(middle_used, 1)

            dve.wait_ge(ld_ids_s, 16)
            mid = ids_s[:, :, NS:NL + 1]
            link(nc.vector.tensor_scalar(mquot[:, 0, :, :], mid, (MR - 1) / 2, 1.0 / MR, ALU.subtract, ALU.mult))
            link(nc.vector.tensor_scalar(mquot[:, 1, :, :], mquot[:, 0, :, :], ROUND, ROUND, ALU.add, ALU.subtract))
            link(nc.vector.scalar_tensor_tensor(out=mlow[:, :, :], in0=mquot[:, 1, :, :], scalar=-float(MR), in1=mid,
                                                op0=ALU.mult, op1=ALU.add))

            def sum_group(g):
                used = GROUPS[g][-1]
                dve.wait_ge(ld_rows[g], 16)
                nc.vector.tensor_reduce(sums[0:used, NM * MR + g * R:NM * MR + (g + 1) * R],
                                        rows[0:used, g % RING, :].rearrange("p (r d) -> p r d", d=DIM), AX.X,
                                        ALU.add).then_inc(rows_used, 1)

            def cut_sums(g0, g1, lo, kinds):
                hi = NM * MR + g1 * R
                link(nc.vector.tensor_copy(sum_parts[:, 0, lo:hi], sums[:, lo:hi]))
                link(nc.vector.tensor_tensor(rest[:, lo:hi], sums[:, lo:hi], sum_parts[:, 0, lo:hi], ALU.subtract))
                link(nc.vector.tensor_copy(sum_parts[:, 1, lo:hi], rest[:, lo:hi]))
                link(nc.vector.tensor_tensor(sum_parts[:, 2, lo:hi], rest[:, lo:hi], sum_parts[:, 1, lo:hi],
                                             ALU.subtract))
                small = sum_parts[:, :, NM * MR:LATE_AT].rearrange("p a (g r) -> p a g r", r=R)
                for ga, gb, fpg, mask in kinds:
                    for f in range(fpg):
                        ins = nc.vector.tensor_scalar(blocks[:, :, ga:gb, f * R:(f + 1) * R], small[:, :, ga:gb, :],
                                                      part_c[:, mask + f:mask + f + 1], None, ALU.mult)
                ins.then_inc(blocks_ready, 1)

            def sum_gathered(s, it, late=0):
                n = 16 * TPC
                dve.wait_ge(gathered_in[s], it * (n * (NGAT - late)) + (n * NGAT - n * late + n * late * EARLY_ROUNDS))
                nc.vector.tensor_reduce(s_raw[:, s, :, NL + late:NF], grows[:, s, :, late:, :], AX.X,
                                        ALU.add).then_inc(grows_used[s], 1)

            for g in range(NG_FIRST):
                sum_group(g)
            dve.wait_ge(rows_used, NG_FIRST)
            dve.wait_ge(middle_used, 2 * NM)
            cut_sums(0, NG_FIRST, 0, [(0, NG_FIRST, FPG_A, MASK_A)])
            for g in range(NG_FIRST, NG):
                sum_group(g)
                if g == NG_FIRST:
                    sum_gathered(0, 0)
            dve.wait_ge(rows_used, NG)
            cut_sums(NG_FIRST, NG, NM * MR + NG_FIRST * R, [(NG_FIRST, NGA, FPG_A, MASK_A), (NGA, NG, FPG_B, MASK_B)])
            dve.wait_ge(ld_pow2, 16)

            def weights_rest(k):
                dve.wait_ge(w_hi_ready, k + 1)
                if k < NZ - 1:
                    nc.vector.tensor_tensor(w1_lo[:, 2 * k:2 * k + 2, :], w1_raw[:, 2 * k:2 * k + 2, :],
                                            w1_hi[:, 2 * k:2 * k + 2, :].bitcast(fp32),
                                            ALU.subtract).then_inc(w_lo_ready, 1)
                elif k == NZ - 1:
                    nc.vector.tensor_tensor(w1_lo[:, KC - 2, :], w1_raw[:, KC - 2, :],
                                            w1_hi[:, KC - 2, :].bitcast(fp32), ALU.subtract)
                    nc.vector.tensor_tensor(w1_lo[0:LAST_K, KC - 1, :], w1_raw[0:LAST_K, KC - 1, :],
                                            w1_hi[0:LAST_K, KC - 1, :].bitcast(fp32),
                                            ALU.subtract).then_inc(w_lo_ready, 1)
                else:
                    nc.vector.tensor_tensor(w2_lo[:, :, :], w2_raw, w2_hi[:, :, :].bitcast(fp32),
                                            ALU.subtract).then_inc(w_lo_ready, 1)

            def pick_bits(c, t, nm=NM, n=1):
                tile = c * TPC + t
                nc.vector.tensor_tensor(
                    bits[:, 0:n, :, :], ids_s[:, bass.ds(tile, n), 0:NS].unsqueeze(3).broadcast_to([P, n, NS, 5]),
                    pow2[:, 0:5].unsqueeze(1).unsqueeze(1).broadcast_to([P, n, NS, 5]),
                    ALU.bitwise_and).then_inc(bits_ready, 1)
                dve.wait_ge(looked_mm, tile + n)
                nc.vector.tensor_tensor(
                    mbits[:, 0:n, 0:nm, :], mlow[:, bass.ds(tile, n), 0:nm].unsqueeze(3).broadcast_to([P, n, nm, 7]),
                    pow2[:, :].unsqueeze(1).unsqueeze(1).broadcast_to([P, n, nm, 7]),
                    ALU.bitwise_and).then_inc(bits_ready, 1)

            def looked_up(nm, n):
                small = X[:, 0:n, 0:NS * R].rearrange("p t (f r) -> p t f r", r=R)
                mid = X[:, 0:n, NS * R:NS * R + nm * MPITCH].rearrange("p t (m r) -> p t m r", r=MPITCH)
                return small, mid

            def pick_levels(lo, hi, nm=NM, n=1):
                small, mid = looked_up(nm, n)
                for level in range(lo, hi):
                    if level == 0:
                        dve.wait_ge(bits_ready, 2)
                    else:
                        dve.wait_ge(middle_step, level)
                    k = 64 >> level
                    w = min(k, MR - k)
                    nc.vector.copy_predicated(
                        mid[:, :, :, 0:w], mbits[:, 0:n, 0:nm, 6 - level:7 - level].broadcast_to([P, n, nm, w]),
                        mid[:, :, :, k:k + w]).then_inc(middle_step, 1)
                    if level < 5:
                        if level > 0:
                            dve.wait_ge(small_step, level)
                        k = 16 >> level
                        nc.vector.copy_predicated(
                            small[:, :, :, 0:k], bits[:, 0:n, :, 4 - level:5 - level].broadcast_to([P, n, NS, k]),
                            small[:, :, :, k:2 * k]).then_inc(small_step, 1)

            def pick_out(s, t, nm=NM, n=1):
                small, mid = looked_up(nm, n)
                dve.wait_ge(small_step, 5)
                nc.vector.tensor_copy(s_raw[:, s, t:t + n, 0:NS], small[:, :, :, 0])
                dve.wait_ge(middle_step, 7)
                nc.vector.tensor_copy(s_raw[:, s, t:t + n, NS:NS + nm], mid[:, :, :, 0]).then_inc(picked, n)
                for step_sem in (bits_ready, small_step, middle_step):
                    nc.vector.sem_clear(step_sem)

            def cut_step_sums(c, s, it):
                dve.wait_ge(picked, (c + 1) * TPC)
                dve.wait_ge(grows_used[s], it + 2)
                first, second, third = (s_cut[:, :, a, :] for a in range(PARTS))
                nc.vector.tensor_copy(first, s_raw[:, s, :, :]).then_inc(cut_step, 1)
                dve.wait_ge(cut_step, c * 3 + 1)
                nc.vector.tensor_tensor(s_rest[:, :, :], s_raw[:, s, :, :], first, ALU.subtract).then_inc(cut_step, 1)
                dve.wait_ge(cut_step, c * 3 + 2)
                nc.vector.tensor_copy(second, s_rest[:, :, :]).then_inc(cut_step, 1)
                dve.wait_ge(cut_step, c * 3 + 3)
                nc.vector.tensor_tensor(third, s_rest[:, :, :], second, ALU.subtract).then_inc(cut_ready, 1)

            def products(c, k, first=False):
                if not first:
                    dve.wait_ge(z_lo_ready, c * NZ + k)
                dve.wait_ge(rowv_ready, c * NZ + k + 1)
                if k < NZ - 1:
                    nc.vector.tensor_tensor(z_raw[:, :, :], rowv[:, :, :],
                                            halves(B_COL), ALU.mult).then_inc(z_ready, 1)
                else:
                    nc.vector.tensor_tensor(z_raw[:, 0, :], rowv[:, 0, :], ps[:, B_COL, 0:CHUNK], ALU.mult)
                    nc.vector.tensor_tensor(z_last[0:LAST_PAIRS, bass.ds(c * CHUNK, CHUNK)], rowv[0:LAST_PAIRS, 1, :],
                                            ps[0:LAST_PAIRS, B_COL, CHUNK:], ALU.mult).then_inc(z_ready, 1)

            def products_rest(c, k):
                dve.wait_ge(z_hi_ready, c * NZ + k + 1)
                if k < NZ - 1:
                    nc.vector.tensor_tensor(z_lo[:, 2 * k:2 * k + 2, :], z_raw[:, :, :],
                                            z_hi[:, 2 * k:2 * k + 2, :].bitcast(fp32),
                                            ALU.subtract).then_inc(z_lo_ready, 1)
                else:
                    nc.vector.tensor_tensor(z_lo[:, KC - 2, :], z_raw[:, 0, :], z_hi[:, KC - 2, :].bitcast(fp32),
                                            ALU.subtract)
                    nc.vector.tensor_tensor(z_lo[0:LAST_K, KC - 1, :], z_last[:, bass.ds(c * CHUNK, CHUNK)],
                                            z_hi[0:LAST_K, KC - 1, :].bitcast(fp32),
                                            ALU.subtract).then_inc(z_lo_ready, 1)

            def hidden_rest(c):
                for pair in range(M1 // 2):
                    dve.wait_ge(h1_hi_ready, c * (M1 // 2) + pair + 1)
                    both = slice(2 * pair, 2 * pair + 2)
                    nc.vector.scalar_tensor_tensor(out=h1_lo[:, both, :], in0=halves(B_H1 + pair), scalar=0.0,
                                                   in1=h1_hi[:, both, :].bitcast(fp32), op0=ALU.max,
                                                   op1=ALU.subtract).then_inc(h1_lo_ready, 1)

            def pick_begin(c, t, nm):
                pick_bits(c, t, nm)
                pick_levels(0, 1, nm)

            def pick_end(s, t, nm):
                pick_levels(3, 7, nm)
                pick_out(s, t, nm)

            def pick_second(c, s, nm=NM):
                products(c, 2)
                pick_begin(c + 1, 1, nm)
                pick_levels(1, 2, nm)
                products_rest(c, 2)
                pick_levels(2, 3, nm)
                pick_end(s, 1, nm)

            def sum_late_piece(i):
                dve.wait_ge(late_pieces, i + 1)
                nc.vector.tensor_reduce(
                    sums[0:MQ, LATE_AT + i * LATE_R:LATE_AT + (i + 1) * LATE_R],
                    late_rows[:, i * LATE_R * DIM:(i + 1) * LATE_R * DIM].rearrange("p (r d) -> p r d", d=DIM),
                    AX.X, ALU.add).then_inc(late_summed, 1)

            def step(c, s_next, it_next, late, late_pieces_here=(), final=False):
                nm = NM + late
                hidden_rest(c - 1)
                pick_begin(c + 1, 0, nm)
                products(c, 0)
                pick_levels(1, 3, nm)
                products_rest(c, 0)
                pick_end(s_next, 0, nm)
                products(c, 1)
                for i in late_pieces_here[:1]:
                    sum_late_piece(i)
                products_rest(c, 1)
                for i in late_pieces_here[1:]:
                    sum_late_piece(i)
                if not final:
                    sum_gathered(s_next, it_next, late)
                pick_second(c, s_next, nm)
                if final:
                    sum_gathered(s_next, it_next, late)
                cut_step_sums(c + 1, s_next, it_next)

            pick_bits(0, 0, n=TPC)
            pick_levels(0, 7, n=TPC)
            pick_out(0, 0, n=TPC)
            cut_step_sums(0, 0, 0)
            weights_rest(0)
            dve.wait_ge(ld_small_w, 16 * NSW)
            sum_late_piece(0)
            products(0, 0, first=True)
            weights_rest(1)
            products_rest(0, 0)
            pick_begin(1, 0, NM)
            products(0, 1)
            pick_levels(1, 3)
            products_rest(0, 1)
            pick_end(1, 0, NM)
            weights_rest(2)
            sum_gathered(1, 0)
            pick_second(0, 1)
            cut_step_sums(1, 1, 0)
            weights_rest(3)
            step(1, 0, 1, 0, (1, 2))
            step(2, 1, 1, 0, (3, 4))
            dve.wait_ge(late_summed, LATE_PIECES)
            late_cols = slice(LATE_AT, NCOL)
            link(nc.vector.tensor_copy(sum_parts[:, 0, late_cols], sums[:, late_cols]))
            link(nc.vector.tensor_tensor(rest[:, late_cols], sums[:, late_cols], sum_parts[:, 0, late_cols],
                                         ALU.subtract))
            link(nc.vector.tensor_copy(sum_parts[:, 1, late_cols], rest[:, late_cols]))
            nc.vector.tensor_tensor(sum_parts[:, 2, late_cols], rest[:, late_cols], sum_parts[:, 1, late_cols],
                                    ALU.subtract).then_inc(late_cut, 1)
            with nc.vector.Fori(EARLY_ROUNDS, ROUNDS - 1) as it:
                for i, s in enumerate((0, 1)):
                    step(it * SLOTS - 1 + i, s, it, 1)
            step(CHUNKS - 3, 0, ROUNDS - 1, 1)
            step(CHUNKS - 2, 1, ROUNDS - 1, 1, final=True)
            hidden_rest(CHUNKS - 2)
            for k in range(NZ):
                products(CHUNKS - 1, k)
                products_rest(CHUNKS - 1, k)
            hidden_rest(CHUNKS - 1)

        @block.tensor
        def _(pe):
            pe.wait_ge(ld_onehot, 16)
            pe.wait_ge(quot_ready, 1)
            with nc.tensor.Fori(0, QB) as b:
                for g, (q, n, first, used) in enumerate(GROUPS):
                    pe.wait_ge(hot_ready, b * NG + g + 1)
                    nc.tensor.matmul(ps[0:used, g, :], onehot_w[:, g, 0:used], quot[:, bass.ds(b * 512, 512)],
                                     start=True, stop=True).then_inc(bcast_ready, 1)
            for m in range(NM):
                for b in range(QB):
                    if m == 0:
                        pe.wait_ge(hot_ready, QB * NG + b + 1)
                    else:
                        pe.wait_ge(mhot_ready, (m - 1) * QB + b + 1)
                    nc.tensor.matmul(ps[0:MQ, b, :], onehot_w[:, NG + m, 0:MQ], quot[:, b * 512:(b + 1) * 512],
                                     start=True, stop=True).then_inc(mbcast_ready, 1)
            for b in range(LATE_QB):
                pe.wait_ge(hot_ready, QB * NG + QB + b + 1)
                at = LATE_FROM * CHUNK + b * 512
                nc.tensor.matmul(ps[0:MQ, QB + b, :], onehot_w[:, NG + NM, 0:MQ], quot[:, at:at + 512],
                                 start=True, stop=True).then_inc(mbcast_ready, 1)
            pe.wait_ge(hot_ready, QB * NG + NG)
            pe.wait_ge(mhot_ready, QB * NM + LATE_QB)

            def look_up_groups(c, t, x, g0, g1):
                at = (c * TPC + t) * P
                for g in range(g0, g1):
                    q, n, first, used = GROUPS[g]
                    for a in range(PARTS):
                        ins = nc.tensor.matmul(x[:, first * R:(first + n) * R], hot[0:used, g, bass.ds(at, P)],
                                               blocks[0:used, a, g, 0:n * R], start=a == 0, stop=a == PARTS - 1)
                return ins

            def look_up_middle(c, t, x):
                at = (c * TPC + t) * P
                for m in range(NM):
                    for a in range(PARTS):
                        nc.tensor.matmul(x[:, NS * R + m * MPITCH:NS * R + m * MPITCH + MR],
                                         hot[0:MQ, NG + m, bass.ds(at, P)],
                                         sum_parts[0:MQ, a, m * MR:(m + 1) * MR], start=a == 0, stop=a == PARTS - 1)

            def look_up_late(c, t, x):
                at = ((c - LATE_FROM) * TPC + t) * P
                to = NS * R + NM * MPITCH
                for a in range(PARTS):
                    nc.tensor.matmul(x[:, to:to + MR], late_hot[0:MQ, bass.ds(at, P)],
                                     sum_parts[0:MQ, a, LATE_AT:NCOL], start=a == 0, stop=a == PARTS - 1)

            def look_up(c, t, late=False):
                if late:
                    look_up_late(c, t, X[:, 0, :])
                look_up_middle(c, t, X[:, 0, :])
                look_up_groups(c, t, X[:, 0, :], 0, NG).then_inc(looked_mm, 1)

            def transpose_sums(c):
                pe.wait_ge(cut_ready, c + 1)
                for t in range(TPC):
                    ins = nc.tensor.matmul(ps[0:SK, B_COL, t * P:(t + 1) * P],
                                           s_cut[:, t, :, :].rearrange("p a f -> p (a f)"), ident[:, :],
                                           start=True, stop=True)
                ins.then_inc(st_ready, 1)

            def select(c, k):
                if k == 0:
                    pe.wait_ge(parts_ready, c + 1)
                else:
                    pe.wait_ge(z_ready, c * NZ + k)
                for side, bank in ((0, B_ROW), (1, B_COL)):
                    for a in range(2):
                        kc = 2 * k + a
                        m = P if kc < KC - 1 else LAST_PAIRS
                        ins = nc.tensor.matmul(ps[0:m, bank, a * CHUNK:(a + 1) * CHUNK],
                                               select_w[:, side, kc * P:kc * P + m], s_parts[:, :],
                                               start=True, stop=True)
                ins.then_inc(select_ready, 1)

            def layer1(c, k):
                pe.wait_ge(z_lo_ready, c * NZ + k + 1)
                for m in range(M1):
                    to = slice(m * P, (m + 1) * P)
                    for kc in (2 * k, 2 * k + 1):
                        n = P if kc < KC - 1 else LAST_K
                        for i, (w, v) in enumerate(((w1_hi, z_hi), (w1_hi, z_lo), (w1_lo, z_hi))):
                            ins = nc.tensor.matmul(ps[:, B_H1 + m // 2, m % 2 * CHUNK:(m % 2 + 1) * CHUNK],
                                                   w[0:n, kc, to], v[0:n, kc, :],
                                                   start=kc == 0 and m % 2 == 0 and i == 0,
                                                   stop=kc == KC - 1 and i == 2, skip_group_check=True)
                    if k == NZ - 1 and m % 2:
                        ins.then_inc(h1_ready, 1)

            def layer2(c):
                pe.wait_ge(y_copied, c + 1)
                for k in range(M1):
                    if k % 2 == 0:
                        pe.wait_ge(h1_lo_ready, c * (M1 // 2) + k // 2 + 1)
                    for m in range(M2):
                        to = slice(m * P, (m + 1) * P)
                        for i, (w, v) in enumerate(((w2_hi, h1_hi), (w2_hi, h1_lo), (w2_lo, h1_hi))):
                            ins = nc.tensor.matmul(ps[:, B_H2, m * CHUNK:(m + 1) * CHUNK], w[:, k, to], v[:, k, :],
                                                   start=k == 0 and m == 0 and i == 0, stop=k == M1 - 1 and i == 2,
                                                   skip_group_check=True)
                ins.then_inc(h2_ready, 1)

            def layer3(c):
                pe.wait_ge(h2_relu, c * M2 + M2)
                for t in range(TPC):
                    for k in range(M2):
                        ins = nc.tensor.matmul(ps[:, B_Y, t:t + 1], h2_s[:, k, t * P:(t + 1) * P], w3_s[:, k:k + 1],
                                               start=k == 0, stop=k == M2 - 1)
                ins.then_inc(y_ready, 1)

            def look_up_second(c, late=False):
                pe.wait_ge(picked, c * TPC + 1)
                look_up(c, 1, late)

            pe.wait_ge(blocks_ready, 1)
            for t in range(TPC):
                look_up_middle(0, t, X[:, t, :])
                look_up_groups(0, t, X[:, t, :], 0, NG_FIRST)
            pe.wait_ge(blocks_ready, 2)
            for t in range(TPC):
                look_up_groups(0, t, X[:, t, :], NG_FIRST, NG).then_inc(looked_mm, 1)
            pe.wait_ge(ld_ident, 16)
            transpose_sums(0)
            pe.wait_ge(ld_select, 16)
            select(0, 0)
            look_up(1, 0)
            select(0, 1)
            pe.wait_ge(w_lo_ready, 1)
            layer1(0, 0)
            pe.wait_ge(w_lo_ready, 2)
            select(0, 2)
            look_up_second(1)
            layer1(0, 1)
            pe.wait_ge(w_lo_ready, 3)
            layer1(0, 2)

            def step(c, late=False):
                transpose_sums(c)
                look_up(c + 1, 0, late)
                select(c, 0)
                layer2(c - 1)
                select(c, 1)
                layer1(c, 0)
                layer3(c - 1)
                select(c, 2)
                look_up_second(c + 1, late)
                layer1(c, 1)
                layer1(c, 2)

            pe.wait_ge(w_lo_ready, 4)
            with nc.tensor.Fori(1, LATE_FROM - 1) as c:
                step(c)
            pe.wait_ge(late_cut, 1)
            with nc.tensor.Fori(LATE_FROM - 1, CHUNKS - 1) as c:
                step(c, late=True)
            transpose_sums(CHUNKS - 1)
            select(CHUNKS - 1, 0)
            layer2(CHUNKS - 2)
            select(CHUNKS - 1, 1)
            layer1(CHUNKS - 1, 0)
            select(CHUNKS - 1, 2)
            layer3(CHUNKS - 2)
            layer1(CHUNKS - 1, 1)
            layer1(CHUNKS - 1, 2)
            layer2(CHUNKS - 1)
            layer3(CHUNKS - 1)


def kernel(**inputs):
    import numpy as np
    import ml_dtypes
    import concourse.bacc as bacc
    from concourse.bass_utils import run_bass_kernel_spmd

    f32 = np.float32
    arrays = {}
    ids = np.ascontiguousarray(inputs["ids"])[:, ORDER]
    by_sample = ids.reshape(TILES, P, NF).transpose(1, 0, 2)
    arrays["ids_sample"] = np.ascontiguousarray(by_sample[:, :, :NL + 1])
    arrays["ids_gather"] = np.ascontiguousarray(by_sample[:, :, NL:])
    arrays["ids_field"] = np.ascontiguousarray(ids[:, :NL + 1].T)

    def filled(f, rows):
        table = np.asarray(inputs[f"tbl_{f}"])
        return np.concatenate([table, table[:rows - table.shape[0]]]).reshape(-1, R * DIM)

    arrays["rows_a"] = np.concatenate([filled(f, Q_A * R) for f in A_FIELDS]).reshape(NGA, P, R * DIM)
    arrays["rows_b"] = np.concatenate([filled(f, Q_B * R) for f in B_FIELDS])
    arrays["medium"] = np.stack([np.asarray(inputs[f"tbl_{f}"]).reshape(MQ, MR * DIM) for f in DENSE_MEDIUM])
    for j, f in enumerate(GATHERED):
        arrays[f"gathered_{j}"] = np.asarray(inputs[f"tbl_{f}"])
    arrays["dense_t"] = np.concatenate([np.asarray(inputs["dense_ctx"]).T, np.ones((1, BATCH), f32)])
    arrays["w1"] = np.concatenate([np.asarray(inputs["W_top1"]), np.asarray(inputs["b_top1"]).reshape(1, H1)])
    arrays["w2"] = np.asarray(inputs["W_top2"])
    arrays["b2"] = np.ascontiguousarray(np.asarray(inputs["b_top2"]).reshape(H2 // P, P).T)
    arrays["w3"] = np.ascontiguousarray(np.asarray(inputs["W_top3"]).reshape(H2 // P, P).T)

    c_field = np.zeros((NL + 1, 2), f32)
    c_field[:, 0], c_field[:, 1] = (R - 1) / 2, 1 / R
    c_field[NS:, 0], c_field[NS:, 1] = (MR - 1) / 2, 1 / MR
    part = np.arange(P)
    c_part = np.zeros((P, NPART), f32)
    c_part[:, NEG_PART], c_part[:, ONE] = -part, 1
    for mask, bias, q, fpg in ((MASK_A, BIAS_A, Q_A, FPG_A), (MASK_B, BIAS_B, Q_B, FPG_B)):
        c_part[:, bias] = 1 - (part % q) ** 2
        for k in range(fpg):
            c_part[:, mask + k] = part // q == k
    c_pow2 = np.tile(2 ** np.arange(7, dtype=np.int32), (P, 1)).astype(np.int32)
    c_onehot = np.zeros((QK, NG + NM + 1, P), np.float16)
    for g, (q, n, first, used) in enumerate(GROUPS):
        for p in range(used):
            h = p % q
            c_onehot[first + p // q, g, p] = 2 * h
            c_onehot[64 + first + p // q, g, p] = -1
    for m in range(NM + 1):
        c_onehot[NS + m, NG + m, :] = 1
    c_select = np.zeros((PARTS, NF, 2, KC * P), f32)
    for n, (i, j) in enumerate(PAIRS):
        c_select[:, POS[i], 0, n] = 1
        c_select[:, POS[j], 1, n] = 1
    arrays["c_field"], arrays["c_part"], arrays["c_pow2"], arrays["c_onehot"] = c_field, c_part, c_pow2, c_onehot
    arrays["c_select"] = c_select.reshape(SK, 2, KC * P).astype(ml_dtypes.bfloat16)
    arrays["c_ident"] = np.eye(P, dtype=f32).astype(ml_dtypes.bfloat16)

    nc = bacc.Bacc("TRN2", target_bir_lowering=False, num_devices=1)
    ap = {n: nc.dram_tensor(n, a.shape, mybir.dt.from_np(a.dtype), kind="ExternalInput").ap()
          for n, a in arrays.items()}
    y = nc.dram_tensor("y_out", (CHUNKS, P, TPC), mybir.dt.float32, kind="ExternalOutput").ap()
    tower(nc, ap["ids_sample"], ap["ids_gather"], ap["ids_field"], ap["rows_a"], ap["rows_b"], ap["medium"],
          [ap[f"gathered_{j}"] for j in range(NGAT)], ap["dense_t"], ap["w1"], ap["w2"], ap["b2"],
          ap["w3"], ap["c_field"], ap["c_part"], ap["c_pow2"], ap["c_onehot"], ap["c_select"], ap["c_ident"], y)
    r = run_bass_kernel_spmd(nc, [arrays], core_ids=[0])
    return r.results[0]["y_out"].transpose(0, 2, 1).reshape(BATCH, 1)
```
